# Optimizing a Trainium2 kernel written in Bass

```python
import numpy as np
import jax
import jax.numpy as jnp

def _softmax(x, axis=-1):
    return jax.nn.softmax(x, axis=axis)
def _gelu(x):
    return jax.nn.gelu(x, approximate=True)
def _silu(x):
    return jax.nn.silu(x)
def _sigmoid(x):
    return jax.nn.sigmoid(x)
def _layernorm(x, axis=-1, eps=1e-5):
    m = jnp.mean(x, axis=axis, keepdims=True)
    v = jnp.var(x, axis=axis, keepdims=True)
    return (x - m) / jnp.sqrt(v + eps)
def _scatter_add(tgt, idx, src, axis=0):
    return tgt.at[idx].add(src)
def _segment_sum(src, seg, n):
    return jax.ops.segment_sum(src, seg, n)

kernel_name = 'mk_adj_ffn_d1_adj_256_fb2ed0'

def setup_inputs(seed: int = 0):
    np.random.seed(seed)
    _w = jnp.asarray
    def _rec_inputs():
        import jax
        import jax.numpy as jnp
        _gk = jax.random.key(seed)
        x = -0.0002928 + 1 * jax.random.normal(jax.random.fold_in(_gk, 1), (64, 256, 256), jnp.float32)
        _a = jax.random.bernoulli(jax.random.fold_in(_gk, 2), 0.015625, (64, 256, 256))
        _a = jnp.logical_or(_a, jnp.swapaxes(_a, -1, -2))
        _a = jnp.logical_or(_a, jnp.eye(256, dtype=bool))
        _af = _a.astype(jnp.float32)
        _af = _af * jax.random.uniform(jax.random.fold_in(_gk, 3), (64, 256, 256), jnp.float32, 0.05, 1)
        adj = _af
        return x, adj
    x, adj = _rec_inputs()
    def _L0_gnn_setup():
        import jax, jax.numpy as jnp
        import numpy as np
        B, N, D, H = (8, 2048, 256, 1024)
        RMS_EPS = 1e-06

        def _rmsnorm(h, w, eps=RMS_EPS):
            var = jnp.mean(jnp.square(h), axis=-1, keepdims=True)
            return h * jax.lax.rsqrt(var + eps) * w
        key = jax.random.key(seed)
        ks = jax.random.split(key, 5)
        x = jax.random.normal(ks[0], (B, N, D), dtype=jnp.float32)
        adjacency = jax.random.uniform(ks[1], (B, N, N), dtype=jnp.float32)
        epsilon = jnp.zeros((), dtype=jnp.float32)
        W1 = jax.random.normal(ks[2], (D, H), dtype=jnp.float32) * (1.0 / np.sqrt(D))
        b1 = jnp.zeros((H,), dtype=jnp.float32)
        rms_weight = jnp.ones((H,), dtype=jnp.float32)
        W2 = jax.random.normal(ks[3], (H, D), dtype=jnp.float32) * (1.0 / np.sqrt(H))
        b2 = jnp.zeros((D,), dtype=jnp.float32)
        return {'x': x, 'adjacency': adjacency, 'epsilon': epsilon, 'W1': W1, 'b1': b1, 'rms_weight': rms_weight, 'W2': W2, 'b2': b2}
    _L0_gnn_all = _L0_gnn_setup()
    _L0_gnn_in = {k: v for k, v in _L0_gnn_all.items() if k in ('epsilon', 'W1', 'b1', 'rms_weight', 'W2', 'b2', )}
    del _L0_gnn_all

    def _L0_ffn_setup():
        import jax, jax.numpy as jnp
        import numpy as np
        B, S, D_MODEL, FFN, P = (8, 4096, 256, 1024, 8)
        BLK = 256
        key = jax.random.key(seed)
        ks = jax.random.split(key, 12)
        x = jax.random.normal(ks[0], (B, S, D_MODEL), jnp.float32)
        Wt = 0.05 * jax.random.normal(ks[1], (FFN, D_MODEL), jnp.float32)
        bt = 0.05 * jax.random.normal(ks[2], (FFN,), jnp.float32)
        sl_cvx = 1.0 + 0.1 * jax.random.normal(ks[3], (FFN, P), jnp.float32)
        of_cvx = 0.1 * jax.random.normal(ks[4], (FFN, P), jnp.float32)
        sl_ccv = 1.0 + 0.1 * jax.random.normal(ks[5], (FFN, P), jnp.float32)
        of_ccv = 0.1 * jax.random.normal(ks[6], (FFN, P), jnp.float32)
        alpha = jnp.zeros((FFN,), jnp.float32)
        Wc = jax.random.normal(ks[7], (D_MODEL, FFN), jnp.float32) / np.sqrt(D_MODEL)
        bc = jnp.zeros((FFN,), jnp.float32)
        Wg = 0.01 * jax.random.normal(ks[8], (D_MODEL, FFN), jnp.float32)
        bg = 2.0 * jnp.ones((FFN,), jnp.float32)
        Wd = jax.random.normal(ks[9], (FFN, D_MODEL), jnp.float32) / np.sqrt(FFN)
        bd = jnp.zeros((D_MODEL,), jnp.float32)
        return {'x': x, 'Wt': Wt, 'bt': bt, 'sl_cvx': sl_cvx, 'of_cvx': of_cvx, 'sl_ccv': sl_ccv, 'of_ccv': of_ccv, 'alpha': alpha, 'Wc': Wc, 'bc': bc, 'Wg': Wg, 'bg': bg, 'Wd': Wd, 'bd': bd}
    _L0_ffn_all = _L0_ffn_setup()
    _L0_ffn_in = {k: v for k, v in _L0_ffn_all.items() if k in ('Wt', 'bt', 'sl_cvx', 'of_cvx', 'sl_ccv', 'of_ccv', 'alpha', 'Wc', 'bc', 'Wg', 'bg', 'Wd', 'bd', )}
    del _L0_ffn_all

    return {
        "x": x,
        "adj": adj,
        "L0_gnn_epsilon": _L0_gnn_in["epsilon"],
        "L0_gnn_W1": _L0_gnn_in["W1"],
        "L0_gnn_b1": _L0_gnn_in["b1"],
        "L0_gnn_rms_weight": _L0_gnn_in["rms_weight"],
        "L0_gnn_W2": _L0_gnn_in["W2"],
        "L0_gnn_b2": _L0_gnn_in["b2"],
        "L0_ffn_Wt": _L0_ffn_in["Wt"],
        "L0_ffn_bt": _L0_ffn_in["bt"],
        "L0_ffn_sl_cvx": _L0_ffn_in["sl_cvx"],
        "L0_ffn_of_cvx": _L0_ffn_in["of_cvx"],
        "L0_ffn_sl_ccv": _L0_ffn_in["sl_ccv"],
        "L0_ffn_of_ccv": _L0_ffn_in["of_ccv"],
        "L0_ffn_alpha": _L0_ffn_in["alpha"],
        "L0_ffn_Wc": _L0_ffn_in["Wc"],
        "L0_ffn_bc": _L0_ffn_in["bc"],
        "L0_ffn_Wg": _L0_ffn_in["Wg"],
        "L0_ffn_bg": _L0_ffn_in["bg"],
        "L0_ffn_Wd": _L0_ffn_in["Wd"],
        "L0_ffn_bd": _L0_ffn_in["bd"],
    }

def reference(x, adj, L0_gnn_epsilon, L0_gnn_W1, L0_gnn_b1, L0_gnn_rms_weight, L0_gnn_W2, L0_gnn_b2, L0_ffn_Wt, L0_ffn_bt, L0_ffn_sl_cvx, L0_ffn_of_cvx, L0_ffn_sl_ccv, L0_ffn_of_ccv, L0_ffn_alpha, L0_ffn_Wc, L0_ffn_bc, L0_ffn_Wg, L0_ffn_bg, L0_ffn_Wd, L0_ffn_bd):
    import jax
    import jax.numpy as jnp
    def _L0_gnn_ref(x, adjacency, epsilon, W1, b1, rms_weight, W2, b2):
        import jax, jax.numpy as jnp
        import numpy as np
        B, N, D, H = (8, 2048, 256, 1024)
        RMS_EPS = 1e-06

        def _rmsnorm(h, w, eps=RMS_EPS):
            var = jnp.mean(jnp.square(h), axis=-1, keepdims=True)
            return h * jax.lax.rsqrt(var + eps) * w
        neighbor_sum = jnp.einsum('bnm,bmd->bnd', adjacency, x)
        agg = epsilon * x + neighbor_sum
        h = jnp.einsum('bnd,dh->bnh', agg, W1) + b1
        h = jax.nn.silu(_rmsnorm(h, rms_weight))
        out = jnp.einsum('bnh,hd->bnd', h, W2) + b2
        return out

    def _L0_ffn_ref(x, Wt, bt, sl_cvx, of_cvx, sl_ccv, of_ccv, alpha, Wc, bc, Wg, bg, Wd, bd):
        import jax, jax.numpy as jnp
        import numpy as np
        B, S, D_MODEL, FFN, P = (8, 4096, 256, 1024, 8)
        BLK = 256
        Bx, Sx, D = x.shape
        T = Bx * Sx
        xf = x.reshape(T, D)
        xb = xf.reshape(T // BLK, BLK, D)
        s = jax.nn.sigmoid(alpha)

        def blk_fn(xx):
            t = jnp.max(xx[:, None, :] + Wt[None, :, :], axis=-1) + bt
            z = t[:, :, None]
            cvx = jnp.max(z * sl_cvx[None] + of_cvx[None], axis=-1)
            ccv = jnp.min(z * sl_ccv[None] + of_ccv[None], axis=-1)
            return s * cvx + (1.0 - s) * ccv
        trop = jax.lax.map(blk_fn, xb).reshape(T, FFN)
        classical = jax.nn.gelu(xf @ Wc + bc, approximate=False)
        g = jax.nn.sigmoid(xf @ Wg + bg)
        fused = g * trop + (1.0 - g) * classical
        out = fused @ Wd + bd
        return out.reshape(Bx, Sx, D)

    x = x + _L0_gnn_ref(_layernorm(x, axis=-1), adj, L0_gnn_epsilon, L0_gnn_W1, L0_gnn_b1, L0_gnn_rms_weight, L0_gnn_W2, L0_gnn_b2)
    x = x + _L0_ffn_ref(_layernorm(x, axis=-1), L0_ffn_Wt, L0_ffn_bt, L0_ffn_sl_cvx, L0_ffn_of_cvx, L0_ffn_sl_ccv, L0_ffn_of_ccv, L0_ffn_alpha, L0_ffn_Wc, L0_ffn_bc, L0_ffn_Wg, L0_ffn_bg, L0_ffn_Wd, L0_ffn_bd)
    return x


_drawn_inputs = setup_inputs


def setup_inputs(seed=0):
    import zlib

    import numpy as np

    out = dict(_drawn_inputs(seed))
    spreads = {'L0_gnn_b1': (0.0, 0.432),
     'L0_gnn_rms_weight': (1.0, 0.2),
     'L0_gnn_b2': (0.0, 0.1),
     'L0_ffn_alpha': (0.0, 0.8),
     'L0_ffn_bc': (0.0, 2.0),
     'L0_ffn_bg': (2.0, 0.2),
     'L0_ffn_bd': (0.0, 0.1)}
    factors = {'L0_ffn_Wt': 3.804,
     'L0_ffn_bt': 3.697,
     'L0_ffn_of_cvx': 4.272,
     'L0_ffn_of_ccv': 3.906,
     'L0_ffn_Wg': 3.492}
    for name, (base, spread) in spreads.items():
        noise = np.random.default_rng([zlib.crc32(name.encode()), seed]).standard_normal(out[name].shape)
        drawn = base * np.exp(spread * noise) if base else spread * noise
        out[name] = jnp.asarray(drawn.astype(out[name].dtype))
    for name, factor in factors.items():
        out[name] = (out[name] * factor).astype(out[name].dtype)
    return out
```

```python
from contextlib import ExitStack

import concourse.bass as bass
from concourse import mybir

P = 128
F32 = mybir.dt.float32
BF16 = mybir.dt.bfloat16
ALU = mybir.AluOpType
ACT = mybir.ActivationFunctionType
ds = bass.ds

LN_EPS = 1e-5
RMS_EPS = 1e-6
UNIT = 32
PARTS = 3
SEL = PARTS * UNIT
ROWS = SEL + PARTS


def steps(eng, n, body):
    body(0, 0, 0)
    body(1, 0, 1)
    if n > 4:
        with eng.Fori(1, n // 2 - 1) as h:
            body(h * 2, h, 0)
            body(h * 2 + 1, h, 1)
    body(n - 2, n // 2 - 1, 0)
    body(n - 1, n // 2 - 1, 1)


def early(i):
    return isinstance(i, int) and i < 2


class Shared:

    def __init__(self, nc, ctx, io):
        self.nc, self.io = nc, io
        self.B, self.N, self.D = io["x"].shape
        self.F = io["L0_gnn_W1"].shape[1]
        self.T = self.B * self.N
        self.FT, self.DH = self.F // P, self.D // P
        self.NT = self.T // P
        self.NP = io["L0_ffn_sl_cvx"].shape[1]

        def sb(name, shape, dt=F32):
            return ctx.enter_context(nc.sbuf_tensor(name, shape, dt))

        def dram(name, shape, dt=F32):
            return nc.dram_tensor(name, shape, dt, kind="Internal").ap()

        T, D, F, FT, NT, NP = self.T, self.D, self.F, self.FT, self.NT, self.NP
        self.x1_d = dram("x1_scratch", [T, D])
        self.xT_d = dram("xT_scratch", [D, T])
        self.xs_d = dram("xs_scratch", [PARTS, D, T], BF16)
        self.dxs_d = dram("dxs_scratch", [PARTS, D, T], BF16)
        self.ws_d = dram("ws_scratch", [PARTS, D, F], BF16)
        self.t_d = dram("t_scratch", [F, T])
        self.ident = sb("ident", [P, P])
        self.wt = sb("wt", [P, FT, D + 1])
        self.b1, self.rw, self.bc, self.bg, self.bt, self.al = (
            sb(n, [P, FT]) for n in ("b1", "rw", "bc", "bg", "bt", "al"))
        self.eps = sb("eps", [P, 1])
        self.coef = sb("coef", [P, 4, FT, NP])
        self.b2, self.bd = sb("b2", [P, D]), sb("bd", [P, D])
        self.mv = sb("mv", [P, NT, 2])
        self.mv2 = sb("mv2", [P, NT, 2])
        self.rstd = sb("rstd", [P, NT])
        self.nt = sb("newton", [P, 2, NT])


def newton_rsqrt(dve, sh, n, var, root, done, at):
    y, z = sh
    dve.reciprocal(y, root).then_inc(done, 1)
    dve.wait_ge(done, at + 1)
    dve.tensor_tensor(z, y, y, ALU.mult).then_inc(done, 1)
    dve.wait_ge(done, at + 2)
    dve.tensor_tensor(z, z, var, ALU.mult).then_inc(done, 1)
    dve.wait_ge(done, at + 3)
    dve.tensor_scalar(z, z, -0.5, 1.5, ALU.mult, ALU.add).then_inc(done, 1)
    dve.wait_ge(done, at + 4)
    dve.tensor_tensor(n, y, z, ALU.mult).then_inc(done, 1)
    dve.wait_ge(done, at + 5)
    return at + 5


def stage_prepare(s):
    nc, io = s.nc, s.io
    D, F, FT, DH, NT, NP = s.D, s.F, s.FT, s.DH, s.NT, s.NP
    XB = 8
    NI = NT // XB
    with ExitStack() as ctx:
        def sb(name, shape, dt=F32):
            return ctx.enter_context(nc.sbuf_tensor(name, shape, dt))

        def sem(name):
            return ctx.enter_context(nc.semaphore(name))

        dwf = sb("p_dw", [P, FT, D])
        part = sb("p_part", [P, PARTS, DH, F], BF16)
        rest = sb("p_rest", [P, DH, F])
        xin = sb("p_x", [P, 2, XB, D])
        stat = sb("p_stat", [P, XB, 6])
        aggr = sb("p_aggr", [P, XB, 2])
        sig = sb("p_sig", [P, 2, FT])
        root = sb("p_root", [P, NT])
        psw = ctx.enter_context(nc.psum_tensor("p_psw", [P, DH, F], F32))
        ld, ldw = sem("p_ld"), sem("p_ldw")
        ldx = [sem("p_ldx0"), sem("p_ldx1")]
        w_done, turned, part_done, rest_done = sem("p_w"), sem("p_turned"), sem("p_part_s"), sem("p_rest_s")
        sig_done, coef_done, st_done, x_used = sem("p_sig_s"), sem("p_coef_s"), sem("p_st"), sem("p_x_used")
        var_done, root_done, ws_out = sem("p_var"), sem("p_root_s"), sem("p_ws_out")
        xv = io["x"].rearrange("b n d -> (b n) d").rearrange("(n p) d -> p n d", p=P)
        NLOAD = 14

        with nc.Block() as block:
            @block.sync
            def _(sp):
                sp.dma_start(s.wt[:, :, 0:D], io["L0_ffn_Wt"].rearrange("(c p) d -> p c d", p=P)).then_inc(ldw, 16)
                sp.dma_start(s.ident[:], io["ident"]).then_inc(ldw, 16)
                with nc.allow_non_contiguous_dma("vectors of f, one value a partition"):
                    sp.dma_start(s.bt[:], io["L0_ffn_bt"].rearrange("(c p) -> p c", p=P)).then_inc(ldw, 16)
                    for dst, name in ((s.b1, "L0_gnn_b1"), (s.rw, "L0_gnn_rms_weight"), (s.bc, "L0_ffn_bc"),
                                      (s.bg, "L0_ffn_bg"), (s.al, "L0_ffn_alpha")):
                        sp.dma_start(dst[:], io[name].rearrange("(c p) -> p c", p=P)).then_inc(ld, 16)
                for n, name in enumerate(("sl_cvx", "of_cvx", "sl_ccv", "of_ccv")):
                    sp.dma_start(s.coef[:, n], io[f"L0_ffn_{name}"].rearrange("(c p) n -> p c n", p=P)).then_inc(ld, 16)
                sp.dma_start(s.b2[:], io["L0_gnn_b2"].partition_broadcast(P)).then_inc(ld, 16)
                sp.dma_start(s.bd[:], io["L0_ffn_bd"].partition_broadcast(P)).then_inc(ld, 16)
                sp.dma_start(s.eps[:], io["L0_gnn_epsilon"].partition_broadcast(P)).then_inc(ld, 16)

                def load(i, h, par):
                    if not early(i):
                        sp.wait_ge(x_used, i - 1)
                    sp.dma_start(xin[:, par], xv[:, ds(i * XB, XB), :]).then_inc(ldx[par], 16)

                steps(sp, NI, load)
                sp.wait_ge(part_done, 3)
                for m in range(PARTS):
                    sp.dma_start(s.ws_d[m].rearrange("(c p) f -> p c f", p=P), part[:, m]).then_inc(ws_out, 16)
                sp.wait_ge(ws_out, 16 * PARTS)

            @block.gpsimd
            def _(pool):
                pool.memset(s.wt[:, :, D:D + 1], 0.0).then_inc(w_done, 1)

            @block.tensor
            def _(pe):
                pe.wait_ge(w_done, 1 + FT + 1)
                for c in range(DH):
                    for f in range(FT):
                        mm = pe.transpose(psw[:, c, f * P:(f + 1) * P], dwf[:, f, c * P:(c + 1) * P], s.ident[:])
                mm.then_inc(turned, 1)

            @block.scalar
            def _(act):
                act.wait_ge(turned, 1)
                act.activation(part[:, 0], psw[:], ACT.Identity).then_inc(part_done, 1)
                act.wait_ge(rest_done, 1)
                act.activation(part[:, 1], rest[:], ACT.Identity).then_inc(part_done, 1)
                act.wait_ge(ld, 16 * (NLOAD - 2))
                act.activation(sig[:, 0], s.al[:], ACT.Sigmoid).then_inc(sig_done, 1)
                act.wait_ge(ld, 16 * (NLOAD - 2))
                act.activation(sig[:, 1], s.al[:], ACT.Sigmoid, scale=-1.0).then_inc(sig_done, 1)
                act.wait_ge(var_done, 1)
                act.activation(root[:], s.nt[:, 0], ACT.Sqrt).then_inc(root_done, 1)

            @block.vector
            def _(dve):
                dve.wait_ge(ldw, 48)
                dve.wait_ge(w_done, 1)
                for f in range(FT):
                    dve.tensor_scalar(s.wt[:, f, 0:D], s.wt[:, f, 0:D], s.bt[:, f:f + 1], None,
                                      ALU.add).then_inc(w_done, 1)
                dve.wait_ge(w_done, 1 + FT)
                dve.tensor_tensor(dwf[:], s.wt[:, :, 0:D], s.wt[:, :, 1:D + 1], ALU.subtract).then_inc(w_done, 1)
                dve.wait_ge(part_done, 1)
                dve.tensor_tensor(rest[:], psw[:], part[:, 0], ALU.subtract).then_inc(rest_done, 1)
                dve.wait_ge(part_done, 2)
                dve.wait_ge(rest_done, 1)
                dve.tensor_tensor(part[:, 2], rest[:], part[:, 1], ALU.subtract).then_inc(part_done, 1)

                dve.wait_ge(sig_done, 2)
                for n in range(4):
                    for f in range(FT):
                        dve.tensor_scalar(s.coef[:, n, f], s.coef[:, n, f], sig[:, n // 2, f:f + 1], None,
                                          ALU.mult).then_inc(coef_done, 1)

                def stats(i, h, par):
                    dve.wait_ge(ldx[par], h * 16 + 16)
                    if not (isinstance(i, int) and i == 0):
                        dve.wait_ge(st_done, i * (2 * XB + 1))
                    for t in range(XB):
                        ins = dve.bn_stats(stat[:, t], xin[:, par, t])
                        ins.then_inc(st_done, 1)
                    dve.wait_ge(st_done, i * (2 * XB + 1) + XB)
                    dve.sem_inc(x_used, 1)
                    for t in range(XB):
                        dve.bn_aggr(aggr[:, t], stat[:, t]).then_inc(st_done, 1)
                    dve.wait_ge(st_done, i * (2 * XB + 1) + 2 * XB)
                    dve.tensor_copy(s.mv[:, ds(i * XB, XB), :], aggr[:]).then_inc(st_done, 1)

                steps(dve, NI, stats)
                dve.wait_ge(st_done, NI * (2 * XB + 1))
                dve.tensor_scalar(s.nt[:, 0], s.mv[:, :, 1], LN_EPS, None, ALU.add).then_inc(var_done, 1)
                dve.wait_ge(var_done, 1)
                dve.wait_ge(root_done, 1)
                newton_rsqrt(dve, (s.nt[:, 1], root[:]), s.rstd[:], s.nt[:, 0], root[:], var_done, 1)


def stage_gnn(s):
    nc, io = s.nc, s.io
    D, F, FT, DH, N = s.D, s.F, s.FT, s.DH, s.N
    G = 2
    R = N // P
    TT = G * R
    W = TT * P
    NI = s.T // W
    with ExitStack() as ctx:
        def sb(name, shape, dt=F32):
            return ctx.enter_context(nc.sbuf_tensor(name, shape, dt))

        def ps(name, shape):
            return ctx.enter_context(nc.psum_tensor(name, shape, F32))

        def sem(name):
            return ctx.enter_context(nc.semaphore(name))

        w1 = sb("g_w1", [P, DH, F])
        w2 = sb("g_w2", [P, FT, D])
        ones = sb("g_ones", [P, P])
        xin = sb("g_x", [P, 2, TT, D])
        adj = sb("g_adj", [P, 2, TT, N])
        xn = sb("g_xn", [P, 2, TT, D])
        xb = sb("g_xb", [P, 2, TT, D])
        adjT = sb("g_adjT", [P, 2, G, R, R, P])
        agg = sb("g_agg", [P, 2, DH, W])
        h = sb("g_h", [P, 2, FT, W])
        sq = sb("g_sq", [P, 2, W])
        sqa = sb("g_sqa", [P, W])
        var = sb("g_var", [P, TT])
        root = sb("g_root", [P, TT])
        rs = sb("g_rs", [P, TT])
        tmp = sb("g_tmp", [P, 2, TT])
        diag = sb("g_diag", [P, TT, P])
        x1 = sb("g_x1", [P, 2, TT, D])
        stat = sb("g_stat", [P, TT, 6])
        aggr = sb("g_aggr", [P, TT, 2])
        ps_h = ps("g_ps_h", [P, 2, W])
        ps_t = ps("g_ps_t", [P, G, R, R, P])
        ps_a = ps("g_ps_a", [P, G, DH, N])
        ps_y = ps("g_ps_y", [P, TT, D])
        ld_w = sem("g_ld_w")
        ld_x, ld_a = [sem("g_ldx0"), sem("g_ldx1")], [sem("g_lda0"), sem("g_lda1")]
        ones_done, xn_done, xb_done = sem("g_ones_s"), sem("g_xn_s"), sem("g_xb_s")
        t_ready, diag_in, side_in = sem("g_t_ready"), sem("g_diag_in"), sem("g_side_in")
        a_ready, agg_done = sem("g_a_ready"), sem("g_agg_s")
        h_ready, h_done, sq_done, sqa_done = sem("g_h_ready"), sem("g_h_s"), sem("g_sq_s"), sem("g_sqa_s")
        ss_ready, root_done, rs_done, diag_done = sem("g_ss"), sem("g_root_s"), sem("g_rs_s"), sem("g_diag_s")
        rb_ready, v_done, silu_done = sem("g_rb"), sem("g_v_s"), sem("g_silu")
        y_ready, x1_done, stat_done = sem("g_y"), sem("g_x1_s"), sem("g_stat_s")
        stats_taken = sem("g_stats_taken")
        x1_out = [sem("g_out0"), sem("g_out1")]
        ps_ss = ps_a[:, G - 1].rearrange("p a b -> p (a b)")
        ps_rb = ps_t[:, 0].rearrange("p m n q -> p (m n q)")
        xv = io["x"].rearrange("b n d -> (b n) d").rearrange("(n p) d -> p n d", p=P)
        av = io["adj"].rearrange("b n m -> (b n) m").rearrange("(n p) m -> p n m", p=P)
        ov = s.x1_d.rearrange("(n p) d -> p n d", p=P)
        RS_STEPS = 6

        def is0(i):
            return isinstance(i, int) and i == 0

        with nc.Block() as block:
            @block.sync
            def _(sp):
                sp.dma_start(w1[:], io["L0_gnn_W1"].rearrange("(c p) f -> p c f", p=P)).then_inc(ld_w, 16)
                sp.dma_start(w2[:], io["L0_gnn_W2"].rearrange("(c p) d -> p c d", p=P)).then_inc(ld_w, 16)

                def store(i, par):
                    sp.wait_ge(x1_done, i + 1)
                    sp.dma_start(ov[:, ds(i * TT, TT), :], x1[:, par]).then_inc(x1_out[par], 16)

                def load(i, hh, par):
                    if not early(i):
                        sp.wait_ge(xn_done, (i - 1) * TT)
                        sp.wait_ge(xb_done, i - 1)
                    sp.dma_start(xin[:, par], xv[:, ds(i * TT, TT), :]).then_inc(ld_x[par], 16)
                    if not early(i):
                        sp.wait_ge(t_ready, (i - 1) * G)
                    sp.dma_start(adj[:, par], av[:, ds(i * TT, TT), :]).then_inc(ld_a[par], 16)
                    if not early(i):
                        store(i - 2, par)

                steps(sp, NI, load)
                store(NI - 2, 0)
                store(NI - 1, 1)
                for par in range(2):
                    sp.wait_ge(x1_out[par], 16 * (NI // 2) + 16)

            @block.gpsimd
            def _(pool):
                pool.memset(ones[:], 1.0).then_inc(ones_done, 1)
                b2 = s.b2[:].unsqueeze(1).to_broadcast([P, TT, D])

                def step(i, hh, par):
                    pool.wait_ge(ld_x[par], hh * 16 + 16)
                    if not early(i):
                        pool.wait_ge(x1_done, i - 1)
                    pool.tensor_tensor(xb[:, par], xin[:, par], b2, ALU.add).then_inc(xb_done, 1)
                    for f in range(1, FT):
                        pool.wait_ge(sq_done, i * FT + f + 1)
                        if f == 1:
                            if not is0(i):
                                pool.wait_ge(ss_ready, i)
                            pool.tensor_tensor(sqa[:], sq[:, 0], sq[:, 1], ALU.add).then_inc(sqa_done, 2)
                        else:
                            pool.wait_ge(sqa_done, i * FT + f)
                            pool.tensor_tensor(sqa[:], sqa[:], sq[:, f % 2], ALU.add).then_inc(sqa_done, 1)

                steps(pool, NI, step)

            @block.tensor
            def _(pe):
                pe.wait_ge(ones_done, 1)

                def turn_adj(i, hh, par):
                    pe.wait_ge(ld_a[par], hh * 16 + 16)
                    if not is0(i):
                        pe.wait_ge(diag_in, i * G)
                        pe.wait_ge(side_in, i * G)
                    if not early(i):
                        pe.wait_ge(v_done, (i - 1) * 2)
                    for g in range(G):
                        for m in range(R):
                            for n in range(R):
                                mm = pe.transpose(ps_t[:, g, m, n], adj[:, par, g * R + n, m * P:(m + 1) * P],
                                                  s.ident[:])
                        mm.then_inc(t_ready, 1)

                def aggregate(i, par):
                    pe.wait_ge(xn_done, (i + 1) * TT)
                    for g in range(G):
                        pe.wait_ge(diag_in, i * G + g + 1)
                        pe.wait_ge(side_in, i * G + g + 1)
                        if g == 0 and not is0(i):
                            pe.wait_ge(agg_done, i * G)
                        if g == G - 1 and not is0(i):
                            pe.wait_ge(rs_done, (i - 1) * RS_STEPS + 1)
                        for c in range(DH):
                            for m in range(R):
                                mm = pe.matmul(ps_a[:, g, c], xn[:, par, g * R + m, c * P:(c + 1) * P],
                                               adjT[:, par, g, m].rearrange("p n q -> p (n q)"),
                                               start=(m == 0), stop=(m == R - 1))
                        mm.then_inc(a_ready, 1)

                def hidden(i, par):
                    pe.wait_ge(agg_done, (i + 1) * G)
                    for f in range(FT):
                        if not (is0(i) and f < 2):
                            pe.wait_ge(h_done, i * FT + (f - 1))
                        for c in range(DH):
                            mm = pe.matmul(ps_h[:, f % 2], w1[:, c, f * P:(f + 1) * P], agg[:, par, c],
                                           start=(c == 0), stop=(c == DH - 1))
                        mm.then_inc(h_ready, 1)

                def squares(i):
                    pe.wait_ge(sqa_done, (i + 1) * FT)
                    pe.wait_ge(agg_done, (i + 1) * G)
                    for t in range(TT):
                        mm = pe.matmul(ps_ss[:, t:t + 1], sqa[:, t * P:(t + 1) * P], ones[:, 0:1],
                                       start=True, stop=True)
                    mm.then_inc(ss_ready, 1)

                def spread(i):
                    pe.wait_ge(diag_done, (i + 1) * TT)
                    for t in range(TT):
                        mm = pe.matmul(ps_rb[:, t * P:(t + 1) * P], ones[:], diag[:, t], start=True, stop=True)
                    mm.then_inc(rb_ready, 1)

                def project(i, par):
                    if not is0(i):
                        pe.wait_ge(x1_done, i)
                    pe.wait_ge(silu_done, (i + 1) * FT)
                    for t in range(TT):
                        for f in range(FT):
                            mm = pe.matmul(ps_y[:, t], h[:, par, f, t * P:(t + 1) * P], w2[:, f],
                                           start=(f == 0), stop=(f == FT - 1))
                    mm.then_inc(y_ready, 1)

                pe.wait_ge(ld_w, 32)
                turn_adj(0, 0, 0)
                aggregate(0, 0)

                def step(i, hh, par):
                    last = isinstance(i, int) and i == NI - 1
                    hidden(i, par)
                    if not last:
                        turn_adj(i + 1, hh + par, 1 - par)
                    if not is0(i):
                        project(i - 1, 1 - par)
                    squares(i)
                    if not last:
                        aggregate(i + 1, 1 - par)
                    spread(i)

                steps(pe, NI, step)
                project(NI - 1, 1)

            @block.scalar
            def _(act):
                def sides(i, par):
                    for g in range(G):
                        act.wait_ge(diag_in, i * G + g + 1)
                        if not early(i):
                            act.wait_ge(a_ready, (i - 1) * G)
                        flat_in = ps_t[:, g].rearrange("p m n q -> p (m n) q")
                        flat_out = adjT[:, par, g].rearrange("p m n q -> p (m n) q")
                        act.activation(flat_out[:, 1:3], flat_in[:, 1:3], ACT.Identity).then_inc(side_in, 1)

                def aggregates(i, par):
                    for g in range(G):
                        act.wait_ge(a_ready, i * G + g + 1)
                        if not early(i):
                            act.wait_ge(h_ready, (i - 1) * FT)
                        act.activation(agg[:, par, :, g * N:(g + 1) * N], ps_a[:, g], ACT.Identity)\
                            .then_inc(agg_done, 1)

                sides(0, 0)
                aggregates(0, 0)

                def step(i, hh, par):
                    last = isinstance(i, int) and i == NI - 1
                    for f in range(FT):
                        act.wait_ge(h_done, i * FT + f + 1)
                        if not (is0(i) and f < 2):
                            act.wait_ge(sqa_done, i * FT + f - 1)
                        act.activation(sq[:, f % 2], h[:, par, f], ACT.Square)\
                            .then_inc(sq_done, 1)
                    if not last:
                        sides(i + 1, 1 - par)
                    act.wait_ge(rs_done, i * RS_STEPS + 1)
                    act.activation(root[:], var[:], ACT.Sqrt).then_inc(root_done, 1)
                    if not last:
                        aggregates(i + 1, 1 - par)
                    for f in range(FT):
                        act.wait_ge(v_done, i * 2 + f // (FT // 2) + 1)
                        act.activation(h[:, par, f], h[:, par, f], ACT.Silu, scale=s.rw[:, f:f + 1])\
                            .then_inc(silu_done, 1)

                steps(act, NI, step)

            @block.vector
            def _(dve):
                def normalise(i, hh, par):
                    dve.wait_ge(ld_x[par], hh * 16 + 16)
                    if not early(i):
                        dve.wait_ge(a_ready, (i - 1) * G)
                    for t in range(TT):
                        dve.tensor_scalar(xn[:, par, t], xin[:, par, t], s.mv[:, ds(i * TT + t, 1), 0],
                                          s.rstd[:, ds(i * TT + t, 1)], ALU.subtract, ALU.mult)\
                            .then_inc(xn_done, 1)

                def diagonals(i, par):
                    for g in range(G):
                        dve.wait_ge(t_ready, i * G + g + 1)
                        if not early(i):
                            dve.wait_ge(a_ready, (i - 1) * G)
                        flat_in = ps_t[:, g].rearrange("p m n q -> p (m n) q")
                        flat_out = adjT[:, par, g].rearrange("p m n q -> p (m n) q")
                        dve.scalar_tensor_tensor(flat_out[:, 0:4:3], s.ident[:].unsqueeze(1).to_broadcast([P, 2, P]),
                                                 s.eps[:], flat_in[:, 0:4:3], ALU.mult, ALU.add)\
                            .then_inc(diag_in, 1)

                for par in range(2):
                    dve.sem_inc(x1_out[par], 16)
                normalise(0, 0, 0)
                diagonals(0, 0)

                def finish(i, hh, par):
                    dve.wait_ge(y_ready, i + 1)
                    dve.wait_ge(xb_done, i + 1)
                    dve.wait_ge(x1_out[par], hh * 16 + 16)
                    dve.tensor_tensor(x1[:, par], ps_y[:], xb[:, par], ALU.add).then_inc(x1_done, 1)
                    dve.wait_ge(x1_done, i + 1)
                    if not is0(i):
                        dve.wait_ge(stat_done, i * (2 * TT + 1))
                    for t in range(TT):
                        dve.bn_stats(stat[:, t], x1[:, par, t]).then_inc(stat_done, 1)
                    dve.wait_ge(stat_done, i * (2 * TT + 1) + TT)
                    dve.sem_inc(stats_taken, 1)
                    for t in range(TT):
                        dve.bn_aggr(aggr[:, t], stat[:, t]).then_inc(stat_done, 1)
                    dve.wait_ge(stat_done, i * (2 * TT + 1) + 2 * TT)
                    dve.tensor_copy(s.mv2[:, ds(i * TT, TT), :], aggr[:]).then_inc(stat_done, 1)

                def step(i, hh, par):
                    last = isinstance(i, int) and i == NI - 1
                    for f in range(FT):
                        dve.wait_ge(h_ready, i * FT + f + 1)
                        if not early(i):
                            dve.wait_ge(y_ready, i - 1)
                        dve.tensor_scalar(h[:, par, f], ps_h[:, f % 2], s.b1[:, f:f + 1], None, ALU.add)\
                            .then_inc(h_done, 1)
                    if not last:
                        normalise(i + 1, hh + par, 1 - par)
                        diagonals(i + 1, 1 - par)
                    if not is0(i):
                        finish(i - 1, hh + par - 1, 1 - par)
                    dve.wait_ge(ss_ready, i + 1)
                    at = i * RS_STEPS
                    dve.tensor_scalar(var[:], ps_ss[:, 0:TT], 1.0 / F, RMS_EPS, ALU.mult, ALU.add).then_inc(rs_done, 1)
                    dve.wait_ge(root_done, i + 1)
                    dve.wait_ge(rs_done, at + 1)
                    if not is0(i):
                        dve.wait_ge(diag_done, i * TT)
                    newton_rsqrt(dve, (tmp[:, 0], tmp[:, 1]), rs[:], var[:], root[:], rs_done, at + 1)
                    if not is0(i):
                        dve.wait_ge(rb_ready, i)
                    for t in range(TT):
                        dve.tensor_scalar(diag[:, t], s.ident[:], rs[:, t:t + 1], None, ALU.mult)\
                            .then_inc(diag_done, 1)
                    dve.wait_ge(rb_ready, i + 1)
                    dve.wait_ge(sq_done, (i + 1) * FT)
                    half = FT // 2
                    rb = ps_rb.unsqueeze(1).to_broadcast([P, half, W])
                    for m in range(2):
                        dve.tensor_tensor(h[:, par, m * half:(m + 1) * half], h[:, par, m * half:(m + 1) * half],
                                          rb, ALU.mult).then_inc(v_done, 1)

                steps(dve, NI, step)
                finish(NI - 1, NI // 2 - 1, 1)


def stage_norm(s):
    nc = s.nc
    D, DH = s.D, s.DH
    TT = 4
    W = TT * P
    NI = s.T // W
    with ExitStack() as ctx:
        def sb(name, shape, dt=F32):
            return ctx.enter_context(nc.sbuf_tensor(name, shape, dt))

        def sem(name):
            return ctx.enter_context(nc.semaphore(name))

        root = sb("n_root", [P, s.NT])
        xin = sb("n_x", [P, 2, TT, D])
        xn = sb("n_xn", [P, 2, TT, D + 1])
        dx = sb("n_dx", [P, 2, TT, D])
        xT = sb("n_xT", [P, 2, DH, W])
        part = sb("n_part", [P, 2, 2, PARTS, DH, W], BF16)
        rest = sb("n_rest", [P, 2, 2, DH, W])
        pst = ctx.enter_context(nc.psum_tensor("n_ps", [P, 2, 2, DH, W], F32))
        ld_x = [sem("n_ldx0"), sem("n_ldx1")]
        out = [sem("n_out0"), sem("n_out1")]
        var_done, root_done, pad_done = sem("n_var"), sem("n_root_s"), sem("n_pad")
        xn_done, dx_done, turned = sem("n_xn_s"), sem("n_dx_s"), sem("n_turned")
        hi_done, mid_done, rest_done, lo_done, xT_done = (
            sem("n_hi"), sem("n_mid"), sem("n_rest_s"), sem("n_lo"), sem("n_xT_s"))
        xv = s.x1_d.rearrange("(n p) d -> p n d", p=P)
        NOUT = 1 + 2 * PARTS

        with nc.Block() as block:
            @block.sync
            def _(sp):
                def store(i, par):
                    sp.wait_ge(lo_done, i * 2 + 2)
                    sp.wait_ge(xT_done, i + 1)
                    sp.dma_start(s.xT_d.rearrange("(c p) t -> p c t", p=P)[:, :, ds(i * W, W)], xT[:, par])\
                        .then_inc(out[par], 16)
                    for k, dst in ((0, s.xs_d), (1, s.dxs_d)):
                        for m in range(PARTS):
                            sp.dma_start(dst[m].rearrange("(c p) t -> p c t", p=P)[:, :, ds(i * W, W)],
                                         part[:, par, k, m]).then_inc(out[par], 16)

                def load(i, h, par):
                    if not early(i):
                        sp.wait_ge(xn_done, (i - 1) * TT)
                    sp.dma_start(xin[:, par], xv[:, ds(i * TT, TT), :]).then_inc(ld_x[par], 16)
                    if not (isinstance(i, int) and i == 0):
                        store(i - 1, 1 - par)

                steps(sp, NI, load)
                store(NI - 1, 1)
                for par in range(2):
                    sp.wait_ge(out[par], 16 * NOUT * (NI // 2))

            @block.gpsimd
            def _(pool):
                for par in range(2):
                    pool.memset(xn[:, par, :, D:D + 1], 0.0).then_inc(pad_done, 1)
                pool.wait_ge(pad_done, 2)

                def step(i, h, par):
                    pool.wait_ge(xn_done, (i + 1) * TT)
                    if not early(i):
                        pool.wait_ge(turned, (i - 1) * 2)
                    pool.tensor_tensor(dx[:, par], xn[:, par, :, 0:D], xn[:, par, :, 1:D + 1], ALU.subtract)\
                        .then_inc(dx_done, 1)

                steps(pool, NI, step)

            @block.tensor
            def _(pe):
                def step(i, h, par):
                    for k in range(2):
                        if k == 0:
                            pe.wait_ge(xn_done, (i + 1) * TT)
                        else:
                            pe.wait_ge(dx_done, i + 1)
                        if not early(i):
                            pe.wait_ge(xT_done, i - 1)
                            pe.wait_ge(rest_done, (i - 1) * 2)
                        src = xn if k == 0 else dx
                        for t in range(TT):
                            for c in range(DH):
                                mm = pe.transpose(pst[:, par, k, c, t * P:(t + 1) * P],
                                                  src[:, par, t, c * P:(c + 1) * P], s.ident[:])
                        mm.then_inc(turned, 1)

                steps(pe, NI, step)

            @block.scalar
            def _(act):
                act.wait_ge(var_done, 1)
                act.activation(root[:], s.nt[:, 0], ACT.Sqrt).then_inc(root_done, 1)

                def step(i, h, par):
                    for k in range(2):
                        act.wait_ge(turned, i * 2 + k + 1)
                        if not early(i):
                            act.wait_ge(out[par], h * (16 * NOUT))
                        act.activation(part[:, par, k, 0], pst[:, par, k], ACT.Identity).then_inc(hi_done, 1)
                        if k == 0:
                            act.activation(xT[:, par], pst[:, par, 0], ACT.Identity).then_inc(xT_done, 1)
                    for k in range(2):
                        act.wait_ge(rest_done, i * 2 + k + 1)
                        act.activation(part[:, par, k, 1], rest[:, par, k], ACT.Identity).then_inc(mid_done, 1)

                steps(act, NI, step)

            @block.vector
            def _(dve):
                dve.tensor_scalar(s.nt[:, 0], s.mv2[:, :, 1], LN_EPS, None, ALU.add).then_inc(var_done, 1)
                dve.wait_ge(root_done, 1)
                dve.wait_ge(var_done, 1)
                newton_rsqrt(dve, (s.nt[:, 1], root[:]), s.rstd[:], s.nt[:, 0], root[:], var_done, 1)

                def normalise(i, h, par):
                    dve.wait_ge(ld_x[par], h * 16 + 16)
                    if not early(i):
                        dve.wait_ge(turned, (i - 1) * 2)
                        dve.wait_ge(dx_done, i - 1)
                    for t in range(TT):
                        dve.tensor_scalar(xn[:, par, t, 0:D], xin[:, par, t], s.mv2[:, ds(i * TT + t, 1), 0],
                                          s.rstd[:, ds(i * TT + t, 1)], ALU.subtract, ALU.mult)\
                            .then_inc(xn_done, 1)

                normalise(0, 0, 0)

                def step(i, h, par):
                    if not (isinstance(i, int) and i == NI - 1):
                        normalise(i + 1, h + par, 1 - par)
                    for k in range(2):
                        dve.wait_ge(hi_done, i * 2 + k + 1)
                        if k == 0:
                            dve.wait_ge(xT_done, i + 1)
                        if not early(i):
                            dve.wait_ge(lo_done, (i - 1) * 2)
                            dve.wait_ge(mid_done, (i - 1) * 2)
                        dve.tensor_tensor(rest[:, par, k], pst[:, par, k], part[:, par, k, 0], ALU.subtract)\
                            .then_inc(rest_done, 1)
                    for k in range(2):
                        dve.wait_ge(mid_done, i * 2 + k + 1)
                        dve.wait_ge(rest_done, i * 2 + k + 1)
                        dve.tensor_tensor(part[:, par, k, 2], rest[:, par, k], part[:, par, k, 1], ALU.subtract)\
                            .then_inc(lo_done, 1)

                steps(dve, NI, step)


def stage_tropical(s):
    nc, io = s.nc, s.io
    D, F, FT = s.D, s.F, s.FT
    NU = D // UNIT
    HALF = 1024
    W = 2 * HALF
    NS = s.T // W
    BANK = 512
    PAIRS = FT // 2
    CH = PAIRS + 1
    VF = FT - 1
    VD = 7
    VL = UNIT - PAIRS * VD
    AT_PAIR = [1, 6, 10, 15, 19, 24, 28]
    AT_LAST = [1, 9, 17, 25]
    assert len(AT_PAIR) == VD and len(AT_LAST) == VL and VD % 2 == 1 and VL % 2 == 0
    HU = UNIT // 2
    with ExitStack() as ctx:
        def sb(name, shape, dt=F32):
            return ctx.enter_context(nc.sbuf_tensor(name, shape, dt))

        def ps(name, shape):
            return ctx.enter_context(nc.psum_tensor(name, shape, F32))

        def sem(name):
            return ctx.enter_context(nc.semaphore(name))

        dxs = sb("t_dxs", [P, NU, W], BF16)
        xs = sb("t_xs", [P, NU, HALF], BF16)
        stat = [sb(f"t_stat{g}", [P, UNIT, P], BF16) for g in range(2)]
        run = sb("t_run", [P, VF, HALF])
        vout = sb("t_vout", [P, VF, HALF])
        aout = [sb(f"t_aout{g}", [P, HALF]) for g in range(2)]
        chain = [ps(f"t_chain{g}", [P, HALF]) for g in range(2)]
        spread = [ps(f"t_spread{b}", [P, HALF]) for b in range(2)]

        const_in, ones_in = sem("t_const"), sem("t_ones")
        x_in, w_in = sem("t_x_in"), [sem("t_w_in0"), sem("t_w_in1")]
        summed = sem("t_summed")
        relued = sem("t_relued")
        fed = sem("t_fed")
        maxed = sem("t_maxed")
        a_out = [sem("t_a_out0"), sem("t_a_out1")]
        v_out = sem("t_v_out")

        def sums_before(st, c, u):
            return st * (CH * D * 2) + c * (D * 2) + u * (UNIT * 2)

        with nc.Block() as block:
            @block.sync
            def _(sp):
                for g in range(2):
                    sp.dma_start(stat[g][0:SEL], io["sel"]).then_inc(const_in, 16)

                def load_x(st, u):
                    for m in range(PARTS):
                        rows = slice(m * UNIT, (m + 1) * UNIT)
                        sp.dma_start(dxs[rows, u, :], s.dxs_d[m, ds(u * UNIT, UNIT), ds(st * W, W)]).then_inc(x_in, 16)
                        sp.dma_start(xs[rows, u, :], s.xs_d[m, ds(u * UNIT, UNIT), ds(st * W + HALF, HALF)])\
                            .then_inc(x_in, 16)

                def load_w(c, u, half):
                    for g in range(2):
                        f = c * 2 + g if c < PAIRS else FT - 1
                        sp.dma_start(stat[g][SEL:ROWS, half * HU:(half + 1) * HU, :],
                                     s.ws_d[:, ds(u * UNIT + half * HU, HU), f * P:(f + 1) * P]).then_inc(w_in[half], 16)

                def store_chain(st, c):
                    for g in range(2):
                        sp.wait_ge(relued, sums_before(st, c, NU) + (g + 1))
                        if c == PAIRS:
                            sp.dma_start(s.t_d[F - P:F, ds(st * W + (HALF + g * BANK), BANK)], aout[g][:, 0:BANK])\
                                .then_inc(a_out[g], 16)
                        else:
                            f = c * 2 + g
                            sp.dma_start(s.t_d[f * P:(f + 1) * P, ds(st * W, HALF)], aout[g][:]).then_inc(a_out[g], 16)

                for u in range(NU):
                    load_x(0, u)
                sp.wait_ge(ones_in, 4)
                for half in range(2):
                    load_w(0, 0, half)

                def step(st, more):
                    for c in range(CH):
                        with sp.Fori(0, NU - 1) as u:
                            for half in range(2):
                                sp.wait_ge(summed, sums_before(st, c, u) + (half + 1) * UNIT)
                                load_w(c, u + 1, half)
                            if c == PAIRS and more:
                                sp.wait_ge(fed, st * D + u * VL + (PAIRS * NU * VD + VL))
                                load_x(st + 1, u)
                        for half in range(2):
                            if c < PAIRS or more:
                                sp.wait_ge(summed, sums_before(st, c, NU - 1) + (half + 1) * UNIT)
                                load_w((c + 1) % CH, 0, half)
                        if c == PAIRS and more:
                            sp.wait_ge(fed, st * D + D)
                            load_x(st + 1, NU - 1)
                        store_chain(st, c)
                    for f in range(VF):
                        sp.wait_ge(maxed, st * (D * VF) + ((D + 1) * VF + f + 1))
                        sp.dma_start(s.t_d[f * P:(f + 1) * P, ds(st * W + HALF, HALF)], vout[:, f]).then_inc(v_out, 16)

                with sp.Fori(0, NS - 1) as st:
                    step(st, True)
                step(NS - 1, False)
                sp.wait_ge(v_out, 16 + NS * VF * 16)
                for g in range(2):
                    sp.wait_ge(a_out[g], 16 + NS * CH * 16)

            @block.gpsimd
            def _(pool):
                pool.memset(dxs[SEL:P], 0.0).then_inc(ones_in, 1)
                for g in range(2):
                    pool.memset(stat[g][SEL:P], 0.0).then_inc(ones_in, 1)
                pool.wait_ge(ones_in, 1)
                pool.memset(dxs[SEL:ROWS], 1.0).then_inc(ones_in, 1)

            @block.tensor
            def _(pe):
                pe.wait_ge(const_in, 32)
                pe.wait_ge(ones_in, 4)

                def unit(st, c, u, last):
                    n0 = pe.snap(sums_before(st, c, u))
                    if last:
                        row0 = pe.snap(st * D + u * VL + PAIRS * NU * VD)
                    else:
                        row0 = pe.snap(st * D + c * (NU * VD) + u * VD)
                    w0 = pe.snap(st * (CH * NU * 32) + c * (NU * 32) + u * 32 + 32)
                    first = isinstance(u, int)
                    at = AT_LAST if last else AT_PAIR
                    for j in range(UNIT):
                        if first and j == 0 and not last:
                            pe.wait_ge(x_in, st * (NU * 2 * PARTS * 16) + NU * 2 * PARTS * 16)
                        if j % HU == 0:
                            pe.wait_ge(w_in[j // HU], w0)
                        for g in range(2):
                            pe.wait_ge(relued, n0 + (2 * j + g + 1))
                            for n in range(1 if last else HALF // BANK):
                                lo = HALF + g * BANK if last else n * BANK
                                mm = pe.matmul(chain[g][:, n * BANK:(n + 1) * BANK], stat[g][:, j, :],
                                               dxs[:, u, lo:lo + BANK],
                                               start=(first and j == 0), stop=True, skip_group_check=True)
                            mm.then_inc(summed, 1)
                        if j in at:
                            i = at.index(j)
                            b = (i + 1) % 2 if last else i % 2
                            used = i + 2 if i == 0 and not last else i + 1
                            pe.wait_ge(maxed, row0 * VF + used * VF)
                            jj = PAIRS * VD + i if last else c * VD + i
                            for n in range(HALF // BANK):
                                mm = pe.matmul(spread[b][:, n * BANK:(n + 1) * BANK], stat[0][0:SEL, jj, :],
                                               xs[0:SEL, u, n * BANK:(n + 1) * BANK], start=True, stop=True)
                            mm.then_inc(fed, 1)

                with pe.Fori(0, NS) as st:
                    with pe.Fori(0, PAIRS) as c:
                        unit(st, c, 0, False)
                        with pe.Fori(1, NU) as u:
                            unit(st, c, u, False)
                    unit(st, PAIRS, 0, True)
                    with pe.Fori(1, NU) as u:
                        unit(st, PAIRS, u, True)

            @block.scalar
            def _(act):
                act.sem_inc(relued, 2)
                for g in range(2):
                    act.sem_inc(a_out[g], 16)

                def unit(st, c, u, last):
                    n0 = act.snap(sums_before(st, c, u))
                    end = isinstance(u, int)
                    w = BANK if last else HALF
                    for j in range(UNIT):
                        for g in range(2):
                            act.wait_ge(summed, n0 + (2 * j + g + 1))
                            if end and j == UNIT - 1:
                                act.wait_ge(a_out[g], st * (CH * 16) + c * 16 + 16)
                                act.activation(aout[g][:, 0:w], chain[g][:, 0:w], ACT.Identity).then_inc(relued, 1)
                            else:
                                act.activation(chain[g][:, 0:w], chain[g][:, 0:w], ACT.Relu).then_inc(relued, 1)

                with act.Fori(0, NS) as st:
                    with act.Fori(0, PAIRS) as c:
                        with act.Fori(0, NU - 1) as u:
                            unit(st, c, u, False)
                        unit(st, c, NU - 1, False)
                    with act.Fori(0, NU - 1) as u:
                        unit(st, PAIRS, u, True)
                    unit(st, PAIRS, NU - 1, True)

            @block.vector
            def _(dve):
                dve.sem_inc(maxed, 2 * VF)
                dve.sem_inc(v_out, 16)

                def unit(st, c, u, last, begin=False, end=False):
                    if last:
                        row0 = dve.snap(st * D + u * VL + PAIRS * NU * VD)
                        d0 = dve.snap(u * UNIT + PAIRS * VD)
                    else:
                        row0 = dve.snap(st * D + c * (NU * VD) + u * VD)
                        d0 = dve.snap(c * VD + u * UNIT)
                    m0 = dve.snap(row0 * VF)
                    for i in range(VL if last else VD):
                        b = (i + 1) % 2 if last else i % 2
                        dve.wait_ge(fed, row0 + (i + 1))
                        for f in range(VF):
                            dve.wait_ge(maxed, m0 + ((i + 1) * VF + f + 1))
                            w = s.wt[:, f, ds(d0 + i, 1)]
                            if begin and i == 0:
                                ins = dve.tensor_scalar(run[:, f], spread[b][:], w, None, ALU.add)
                            elif end and i == VL - 1:
                                if f == 0:
                                    dve.wait_ge(v_out, st * (VF * 16) + 16)
                                ins = dve.scalar_tensor_tensor(vout[:, f], spread[b][:], w, run[:, f], ALU.add, ALU.max)
                            else:
                                ins = dve.scalar_tensor_tensor(run[:, f], spread[b][:], w, run[:, f], ALU.add, ALU.max)
                            ins.then_inc(maxed, 1)

                with dve.Fori(0, NS) as st:
                    unit(st, 0, 0, False, begin=True)
                    with dve.Fori(1, NU) as u:
                        unit(st, 0, u, False)
                    with dve.Fori(1, PAIRS) as c:
                        with dve.Fori(0, NU) as u:
                            unit(st, c, u, False)
                    with dve.Fori(0, NU - 1) as u:
                        unit(st, PAIRS, u, True)
                    unit(st, PAIRS, NU - 1, True, end=True)


def stage_ffn(s):
    nc, io = s.nc, s.io
    D, F, FT, DH, NP = s.D, s.F, s.FT, s.DH, s.NP
    TT = 8
    W = TT * P
    BANK = 512
    NI = s.T // W
    TR = 4
    AR = NP - 1
    Q = 2 * (NP - 1)
    DV = Q + 4
    with ExitStack() as ctx:
        def sb(name, shape, dt=F32):
            return ctx.enter_context(nc.sbuf_tensor(name, shape, dt))

        def ps(name, shape):
            return ctx.enter_context(nc.psum_tensor(name, shape, F32))

        def sem(name):
            return ctx.enter_context(nc.semaphore(name))

        wc, wg = sb("f_wc", [P, DH, F]), sb("f_wg", [P, DH, F])
        wd = sb("f_wd", [P, FT, D])
        xT = sb("f_xT", [P, 2, DH, W])
        x1 = sb("f_x1", [P, 2, TT, D])
        t = sb("f_t", [P, TR, W])
        cl = sb("f_cl", [P, 2, FT, W])
        gate = sb("f_gate", [P, 2, W])
        acc = sb("f_acc", [P, 2, 2, W])
        piece = sb("f_piece", [P, AR, W])
        ps_h = ps("f_ps_h", [P, 2, W])
        ps_o = ps("f_ps_o", [P, TT, D])
        ld_w = sem("f_ld_w")
        ld_xT = [sem("f_ldxT0"), sem("f_ldxT1")]
        ld_x1 = [sem("f_ldx10"), sem("f_ldx11")]
        ld_t = [sem(f"f_ldt{r}") for r in range(TR)]
        h_ready, h_read = sem("f_h_ready"), sem("f_h_read")
        aff_done, alu_done, fused = sem("f_aff"), sem("f_alu"), sem("f_fused")
        o_ready, o_done, bias_done = sem("f_o_ready"), sem("f_o_done"), sem("f_bias")
        out = [sem("f_out0"), sem("f_out1")]
        x1v = s.x1_d.rearrange("(n p) d -> p n d", p=P)
        ov = io["out"].rearrange("b n d -> (b n) d").rearrange("(n p) d -> p n d", p=P)
        xTv = s.xT_d.rearrange("(c p) t -> p c t", p=P)

        def is0(i):
            return isinstance(i, int) and i == 0

        with nc.Block() as block:
            @block.sync
            def _(sp):
                sp.dma_start(wc[:], io["L0_ffn_Wc"].rearrange("(c p) f -> p c f", p=P)).then_inc(ld_w, 16)
                sp.dma_start(wg[:], io["L0_ffn_Wg"].rearrange("(c p) f -> p c f", p=P)).then_inc(ld_w, 16)
                sp.dma_start(wd[:], io["L0_ffn_Wd"].rearrange("(c p) d -> p c d", p=P)).then_inc(ld_w, 16)

                def load_xT(i, h, par):
                    if not early(i):
                        sp.wait_ge(h_ready, (i - 1) * (2 * FT))
                    sp.dma_start(xT[:, par], xTv[:, :, ds(i * W, W)]).then_inc(ld_xT[par], 16)

                def store(i, par):
                    sp.wait_ge(o_done, i + 1)
                    sp.dma_start(ov[:, ds(i * TT, TT), :], x1[:, par]).then_inc(out[par], 16)

                load_xT(0, 0, 0)

                def step(i, h, par):
                    if not early(i):
                        sp.wait_ge(out[par], h * 16)
                    sp.dma_start(x1[:, par], x1v[:, ds(i * TT, TT), :]).then_inc(ld_x1[par], 16)
                    for f in range(FT):
                        if not (is0(i) and f < TR):
                            sp.wait_ge(aff_done, (i * FT + f - TR + 1) * (2 * NP))
                        sp.dma_start(t[:, f % TR], s.t_d[f * P:(f + 1) * P, ds(i * W, W)]).then_inc(ld_t[f % TR], 16)
                        if f == 0 and not (isinstance(i, int) and i == NI - 1):
                            load_xT(i + 1, h + par, 1 - par)
                    if not is0(i):
                        store(i - 1, 1 - par)

                steps(sp, NI, step)
                store(NI - 1, 1)
                for par in range(2):
                    sp.wait_ge(out[par], 16 * (NI // 2))

            @block.gpsimd
            def _(pool):
                bd = s.bd[:].unsqueeze(1).to_broadcast([P, TT, D])

                def step(i, h, par):
                    pool.wait_ge(ld_x1[par], h * 16 + 16)
                    pool.tensor_tensor(x1[:, par], x1[:, par], bd, ALU.add).then_inc(bias_done, 1)

                steps(pool, NI, step)

            @block.tensor
            def _(pe):
                pe.wait_ge(ld_w, 48)

                def product(n, w, f, par, slot, fresh):
                    if not fresh:
                        pe.wait_ge(h_read, n - 1)
                    for b in range(W // BANK):
                        for c in range(DH):
                            mm = pe.matmul(ps_h[:, slot, b * BANK:(b + 1) * BANK], w[:, c, f * P:(f + 1) * P],
                                           xT[:, par, c, b * BANK:(b + 1) * BANK], start=(c == 0), stop=(c == DH - 1))
                    mm.then_inc(h_ready, 1)

                def down(i, par, k):
                    if k == 0:
                        pe.wait_ge(fused, (i + 1) * FT)
                        if not is0(i):
                            pe.wait_ge(o_done, i)
                    for f in range(FT):
                        mm = pe.matmul(ps_o[:, k], cl[:, par, f, k * P:(k + 1) * P], wd[:, f],
                                       start=(f == 0), stop=(f == FT - 1))
                    if k == TT - 1:
                        mm.then_inc(o_ready, 1)

                def step(i, h, par):
                    pe.wait_ge(ld_xT[par], h * 16 + 16)
                    for f in range(FT):
                        product(i * (2 * FT) + f, wc, f, par, f % 2, is0(i) and f < 2)
                    for f in range(FT):
                        product(i * (2 * FT) + (FT + f), wg, f, par, f % 2, False)
                        if not is0(i):
                            down(i - 1, 1 - par, f)

                steps(pe, NI, step)
                for k in range(TT):
                    down(NI - 1, 1, k)

            @block.scalar
            def _(act):
                def step(i, h, par):
                    for f in range(FT):
                        act.wait_ge(h_ready, i * (2 * FT) + f + 1)
                        if f == 0 and not early(i):
                            act.wait_ge(o_ready, i - 1)
                        act.activation(cl[:, par, f], ps_h[:, f % 2], ACT.Gelu, bias=s.bc[:, f:f + 1])\
                            .then_inc(h_read, 1)
                    for f in range(FT):
                        n = i * FT + f
                        act.wait_ge(h_ready, i * (2 * FT) + (FT + f + 1))
                        if not (is0(i) and f < 2):
                            act.wait_ge(fused, n - 1)
                        act.activation(gate[:, f % 2], ps_h[:, f % 2], ACT.Sigmoid, bias=s.bg[:, f:f + 1])\
                            .then_inc(h_read, 1)
                        act.wait_ge(ld_t[f % TR], i * (FT // TR * 16) + (f // TR * 16 + 16))
                        for p in range(NP):
                            for side in range(2):
                                q = (p - 1) * 2 + side
                                if p == 0:
                                    dst = acc[:, f % 2, side]
                                else:
                                    dst = piece[:, q % AR]
                                    if not (is0(i) and f == 0 and q < AR):
                                        if q < AR:
                                            act.wait_ge(alu_done, (n - 1) * DV + (q + AR + 1))
                                        else:
                                            act.wait_ge(alu_done, n * DV + (q - AR + 1))
                                act.activation(dst, t[:, f % TR], ACT.Identity,
                                               bias=s.coef[:, 2 * side + 1, f, p:p + 1],
                                               scale=s.coef[:, 2 * side, f, p:p + 1]).then_inc(aff_done, 1)

                steps(act, NI, step)

            @block.vector
            def _(dve):
                def step(i, h, par):
                    for f in range(FT):
                        n = i * FT + f
                        a0, d0 = n * (2 * NP), n * DV
                        cvx, ccv = acc[:, f % 2, 0], acc[:, f % 2, 1]
                        for q in range(Q):
                            dve.wait_ge(aff_done, a0 + (2 + q + 1))
                            if q >= 2:
                                dve.wait_ge(alu_done, d0 + (q - 1))
                            a = acc[:, f % 2, q % 2]
                            dve.tensor_tensor(a, a, piece[:, q % AR], ALU.max if q % 2 == 0 else ALU.min)\
                                .then_inc(alu_done, 1)
                        dve.wait_ge(alu_done, d0 + Q)
                        dve.tensor_tensor(cvx, cvx, ccv, ALU.add).then_inc(alu_done, 1)
                        dve.wait_ge(alu_done, d0 + (Q + 1))
                        dve.wait_ge(h_read, i * (2 * FT) + (FT + f + 1))
                        dve.tensor_tensor(cvx, cvx, cl[:, par, f], ALU.subtract).then_inc(alu_done, 1)
                        dve.wait_ge(alu_done, d0 + (Q + 2))
                        dve.tensor_tensor(cvx, cvx, gate[:, f % 2], ALU.mult).then_inc(alu_done, 1)
                        dve.wait_ge(alu_done, d0 + (Q + 3))
                        dve.tensor_tensor(cl[:, par, f], cl[:, par, f], cvx, ALU.add).then_inc(alu_done, 1)
                        dve.wait_ge(alu_done, d0 + (Q + 4))
                        dve.sem_inc(fused, 1)
                    if not is0(i):
                        finish(i - 1, 1 - par)

                def finish(i, par):
                    dve.wait_ge(o_ready, i + 1)
                    dve.wait_ge(bias_done, i + 1)
                    dve.tensor_tensor(x1[:, par], ps_o[:], x1[:, par], ALU.add).then_inc(o_done, 1)

                steps(dve, NI, step)
                finish(NI - 1, 1)


def build(nc, io):
    with ExitStack() as ctx:
        s = Shared(nc, ctx, io)
        stage_prepare(s)
        stage_gnn(s)
        stage_norm(s)
        stage_tropical(s)
        stage_ffn(s)


def kernel(**inputs):
    import ml_dtypes
    import numpy as np
    import concourse.bacc as bacc
    from concourse.bass_utils import run_bass_kernel_spmd

    arrays = {name: np.ascontiguousarray(a) for name, a in inputs.items()}
    for name, a in arrays.items():
        if a.ndim == 0:
            arrays[name] = a.reshape(1)
    arrays["ident"] = np.eye(P, dtype=np.float32)
    arrays["sel"] = np.ascontiguousarray(np.broadcast_to(
        np.tile(np.eye(UNIT), (PARTS, 1))[:, :, None], (SEL, UNIT, P))).astype(ml_dtypes.bfloat16)
    nc = bacc.Bacc("TRN2", target_bir_lowering=False, num_devices=1)
    io = {name: nc.dram_tensor(f"in_{name}", a.shape, mybir.dt.from_np(a.dtype), kind="ExternalInput").ap()
          for name, a in arrays.items()}
    io["out"] = nc.dram_tensor("out_x", arrays["x"].shape, F32, kind="ExternalOutput").ap()
    build(nc, io)
    r = run_bass_kernel_spmd(nc, [{f"in_{name}": a for name, a in arrays.items()}], core_ids=[0])
    return r.results[0]["out_x"]
```

```python
from contextlib import ExitStack

import concourse.bass as bass
from concourse import mybir

P = 128
F32 = mybir.dt.float32
BF16 = mybir.dt.bfloat16
ALU = mybir.AluOpType
ACT = mybir.ActivationFunctionType
ds = bass.ds

LN_EPS = 1e-5
RMS_EPS = 1e-6
UNIT = 32
PARTS = 3
SEL = PARTS * UNIT
ROWS = SEL + PARTS


def steps(eng, n, body):
    body(0, 0, 0)
    body(1, 0, 1)
    if n > 4:
        with eng.Fori(1, n // 2 - 1) as h:
            body(h * 2, h, 0)
            body(h * 2 + 1, h, 1)
    body(n - 2, n // 2 - 1, 0)
    body(n - 1, n // 2 - 1, 1)


def early(i):
    return isinstance(i, int) and i < 2


class Shared:

    def __init__(self, nc, ctx, io):
        self.nc, self.io = nc, io
        self.B, self.N, self.D = io["x"].shape
        self.F = io["L0_gnn_W1"].shape[1]
        self.T = self.B * self.N
        self.FT, self.DH = self.F // P, self.D // P
        self.NT = self.T // P
        self.NP = io["L0_ffn_sl_cvx"].shape[1]

        def sb(name, shape, dt=F32):
            return ctx.enter_context(nc.sbuf_tensor(name, shape, dt))

        def dram(name, shape, dt=F32):
            return nc.dram_tensor(name, shape, dt, kind="Internal").ap()

        T, D, F, FT, NT, NP = self.T, self.D, self.F, self.FT, self.NT, self.NP
        self.x1_d = dram("x1_scratch", [T, D])
        self.xT_d = dram("xT_scratch", [D, T])
        self.dxs_d = dram("dxs_scratch", [PARTS, D, T], BF16)
        self.PAIRS = FT // 2
        self.CH = self.PAIRS + 1
        self.ws_d = dram("ws_scratch", [PARTS, self.CH * 2, D, P], BF16)
        self.t_d = dram("t_scratch", [F, T])
        self.ident = sb("ident", [P, P])
        self.wt = sb("wt", [P, FT, D + 1])
        self.b1, self.rw, self.bc, self.bg, self.bt, self.al = (
            sb(n, [P, FT]) for n in ("b1", "rw", "bc", "bg", "bt", "al"))
        self.eps = sb("eps", [P, 1])
        self.coef = sb("coef", [P, 4, FT, NP])
        self.b2, self.bd = sb("b2", [P, D]), sb("bd", [P, D])
        self.mv = sb("mv", [P, NT, 2])
        self.mv2 = sb("mv2", [P, NT, 2])
        self.rstd = sb("rstd", [P, NT])
        self.nt = sb("newton", [P, 2, NT])


def newton_rsqrt(dve, sh, n, var, root, done, at):
    y, z = sh
    dve.reciprocal(y, root).then_inc(done, 1)
    dve.wait_ge(done, at + 1)
    dve.tensor_tensor(z, y, y, ALU.mult).then_inc(done, 1)
    dve.wait_ge(done, at + 2)
    dve.tensor_tensor(z, z, var, ALU.mult).then_inc(done, 1)
    dve.wait_ge(done, at + 3)
    dve.tensor_scalar(z, z, -0.5, 1.5, ALU.mult, ALU.add).then_inc(done, 1)
    dve.wait_ge(done, at + 4)
    dve.tensor_tensor(n, y, z, ALU.mult).then_inc(done, 1)
    dve.wait_ge(done, at + 5)
    return at + 5


def stage_prepare(s):
    nc, io = s.nc, s.io
    D, F, FT, DH, NT, NP = s.D, s.F, s.FT, s.DH, s.NT, s.NP
    XB = 8
    NI = NT // XB
    with ExitStack() as ctx:
        def sb(name, shape, dt=F32):
            return ctx.enter_context(nc.sbuf_tensor(name, shape, dt))

        def sem(name):
            return ctx.enter_context(nc.semaphore(name))

        dwf = sb("p_dw", [P, FT, D])
        part = sb("p_part", [P, PARTS, DH, F], BF16)
        rest = sb("p_rest", [P, DH, F])
        xin = sb("p_x", [P, 2, XB, D])
        stat = sb("p_stat", [P, XB, 6])
        aggr = sb("p_aggr", [P, XB, 2])
        sig = sb("p_sig", [P, 2, FT])
        root = sb("p_root", [P, NT])
        psw = ctx.enter_context(nc.psum_tensor("p_psw", [P, DH, F], F32))
        ld, ldw = sem("p_ld"), sem("p_ldw")
        ldx = [sem("p_ldx0"), sem("p_ldx1")]
        w_done, turned, part_done, rest_done = sem("p_w"), sem("p_turned"), sem("p_part_s"), sem("p_rest_s")
        sig_done, coef_done, st_done, x_used = sem("p_sig_s"), sem("p_coef_s"), sem("p_st"), sem("p_x_used")
        var_done, root_done, ws_out = sem("p_var"), sem("p_root_s"), sem("p_ws_out")
        xv = io["x"].rearrange("b n d -> (b n) d").rearrange("(n p) d -> p n d", p=P)
        NLOAD = 14

        with nc.Block() as block:
            @block.sync
            def _(sp):
                sp.dma_start(s.wt[:, :, 0:D], io["L0_ffn_Wt"].rearrange("(c p) d -> p c d", p=P)).then_inc(ldw, 16)
                sp.dma_start(s.ident[:], io["ident"]).then_inc(ldw, 16)
                with nc.allow_non_contiguous_dma("vectors of f, one value a partition"):
                    sp.dma_start(s.bt[:], io["L0_ffn_bt"].rearrange("(c p) -> p c", p=P)).then_inc(ldw, 16)
                    for dst, name in ((s.b1, "L0_gnn_b1"), (s.rw, "L0_gnn_rms_weight"), (s.bc, "L0_ffn_bc"),
                                      (s.bg, "L0_ffn_bg"), (s.al, "L0_ffn_alpha")):
                        sp.dma_start(dst[:], io[name].rearrange("(c p) -> p c", p=P)).then_inc(ld, 16)
                for n, name in enumerate(("sl_cvx", "of_cvx", "sl_ccv", "of_ccv")):
                    sp.dma_start(s.coef[:, n], io[f"L0_ffn_{name}"].rearrange("(c p) n -> p c n", p=P)).then_inc(ld, 16)
                sp.dma_start(s.b2[:], io["L0_gnn_b2"].partition_broadcast(P)).then_inc(ld, 16)
                sp.dma_start(s.bd[:], io["L0_ffn_bd"].partition_broadcast(P)).then_inc(ld, 16)
                sp.dma_start(s.eps[:], io["L0_gnn_epsilon"].partition_broadcast(P)).then_inc(ld, 16)

                def load(i, h, par):
                    if not early(i):
                        sp.wait_ge(x_used, i - 1)
                    sp.dma_start(xin[:, par], xv[:, ds(i * XB, XB), :]).then_inc(ldx[par], 16)

                steps(sp, NI, load)
                sp.wait_ge(part_done, 3)
                for m in range(PARTS):
                    for c in range(DH):
                        rows = slice(c * P, (c + 1) * P)
                        sp.dma_start(s.ws_d[m, 0:FT, rows, :].rearrange("n p f -> p n f"),
                                     part[:, m, c].rearrange("p (n f) -> p n f", f=P)).then_inc(ws_out, 16)
                        for g in range(2):
                            sp.dma_start(s.ws_d[m, FT + g, rows, :], part[:, m, c, F - P:F]).then_inc(ws_out, 16)
                sp.wait_ge(ws_out, 16 * PARTS * DH * 3)

            @block.gpsimd
            def _(pool):
                pool.memset(s.wt[:, :, D:D + 1], 0.0).then_inc(w_done, 1)

            @block.tensor
            def _(pe):
                pe.wait_ge(w_done, 1 + FT + 1)
                for c in range(DH):
                    for f in range(FT):
                        mm = pe.transpose(psw[:, c, f * P:(f + 1) * P], dwf[:, f, c * P:(c + 1) * P], s.ident[:])
                mm.then_inc(turned, 1)

            @block.scalar
            def _(act):
                act.wait_ge(turned, 1)
                act.activation(part[:, 0], psw[:], ACT.Identity).then_inc(part_done, 1)
                act.wait_ge(rest_done, 1)
                act.activation(part[:, 1], rest[:], ACT.Identity).then_inc(part_done, 1)
                act.wait_ge(ld, 16 * (NLOAD - 2))
                act.activation(sig[:, 0], s.al[:], ACT.Sigmoid).then_inc(sig_done, 1)
                act.wait_ge(ld, 16 * (NLOAD - 2))
                act.activation(sig[:, 1], s.al[:], ACT.Sigmoid, scale=-1.0).then_inc(sig_done, 1)
                act.wait_ge(var_done, 1)
                act.activation(root[:], s.nt[:, 0], ACT.Sqrt).then_inc(root_done, 1)

            @block.vector
            def _(dve):
                dve.wait_ge(ldw, 48)
                dve.wait_ge(w_done, 1)
                for f in range(FT):
                    dve.tensor_scalar(s.wt[:, f, 0:D], s.wt[:, f, 0:D], s.bt[:, f:f + 1], None,
                                      ALU.add).then_inc(w_done, 1)
                dve.wait_ge(w_done, 1 + FT)
                dve.tensor_tensor(dwf[:], s.wt[:, :, 0:D], s.wt[:, :, 1:D + 1], ALU.subtract).then_inc(w_done, 1)
                dve.wait_ge(part_done, 1)
                dve.tensor_tensor(rest[:], psw[:], part[:, 0], ALU.subtract).then_inc(rest_done, 1)
                dve.wait_ge(part_done, 2)
                dve.wait_ge(rest_done, 1)
                dve.tensor_tensor(part[:, 2], rest[:], part[:, 1], ALU.subtract).then_inc(part_done, 1)

                dve.wait_ge(sig_done, 2)
                for n in range(4):
                    for f in range(FT):
                        dve.tensor_scalar(s.coef[:, n, f], s.coef[:, n, f], sig[:, n // 2, f:f + 1], None,
                                          ALU.mult).then_inc(coef_done, 1)

                def stats(i, h, par):
                    dve.wait_ge(ldx[par], h * 16 + 16)
                    if not (isinstance(i, int) and i == 0):
                        dve.wait_ge(st_done, i * (2 * XB + 1))
                    for t in range(XB):
                        ins = dve.bn_stats(stat[:, t], xin[:, par, t])
                        ins.then_inc(st_done, 1)
                    dve.wait_ge(st_done, i * (2 * XB + 1) + XB)
                    dve.sem_inc(x_used, 1)
                    for t in range(XB):
                        dve.bn_aggr(aggr[:, t], stat[:, t]).then_inc(st_done, 1)
                    dve.wait_ge(st_done, i * (2 * XB + 1) + 2 * XB)
                    dve.tensor_copy(s.mv[:, ds(i * XB, XB), :], aggr[:]).then_inc(st_done, 1)

                steps(dve, NI, stats)
                dve.wait_ge(st_done, NI * (2 * XB + 1))
                dve.tensor_scalar(s.nt[:, 0], s.mv[:, :, 1], LN_EPS, None, ALU.add).then_inc(var_done, 1)
                dve.wait_ge(var_done, 1)
                dve.wait_ge(root_done, 1)
                newton_rsqrt(dve, (s.nt[:, 1], root[:]), s.rstd[:], s.nt[:, 0], root[:], var_done, 1)


def stage_gnn(s):
    nc, io = s.nc, s.io
    D, F, FT, DH, N = s.D, s.F, s.FT, s.DH, s.N
    G = 2
    R = N // P
    TT = G * R
    W = TT * P
    NI = s.T // W
    with ExitStack() as ctx:
        def sb(name, shape, dt=F32):
            return ctx.enter_context(nc.sbuf_tensor(name, shape, dt))

        def ps(name, shape):
            return ctx.enter_context(nc.psum_tensor(name, shape, F32))

        def sem(name):
            return ctx.enter_context(nc.semaphore(name))

        w1 = sb("g_w1", [P, DH, F])
        w2 = sb("g_w2", [P, FT, D])
        ones = sb("g_ones", [P, P])
        xin = sb("g_x", [P, 2, TT, D])
        adj = sb("g_adj", [P, 2, TT, N])
        xn = sb("g_xn", [P, 2, TT, D])
        xb = sb("g_xb", [P, 2, TT, D])
        adjT = sb("g_adjT", [P, 2, G, R, R, P])
        agg = sb("g_agg", [P, 2, DH, W])
        h = sb("g_h", [P, 2, FT, W])
        sq = sb("g_sq", [P, 2, W])
        sqa = sb("g_sqa", [P, W])
        var = sb("g_var", [P, TT])
        root = sb("g_root", [P, TT])
        rs = sb("g_rs", [P, TT])
        tmp = sb("g_tmp", [P, 2, TT])
        diag = sb("g_diag", [P, TT, P])
        x1 = sb("g_x1", [P, 2, TT, D])
        stat = sb("g_stat", [P, TT, 6])
        aggr = sb("g_aggr", [P, TT, 2])
        ps_h = ps("g_ps_h", [P, 2, W])
        ps_t = ps("g_ps_t", [P, G, R, R, P])
        ps_a = ps("g_ps_a", [P, G, DH, N])
        ps_y = ps("g_ps_y", [P, TT, D])
        ld_w = sem("g_ld_w")
        ld_x, ld_a = [sem("g_ldx0"), sem("g_ldx1")], [sem("g_lda0"), sem("g_lda1")]
        ones_done, xn_done, xb_done = sem("g_ones_s"), sem("g_xn_s"), sem("g_xb_s")
        t_ready, diag_in, side_in = sem("g_t_ready"), sem("g_diag_in"), sem("g_side_in")
        a_ready, agg_done = sem("g_a_ready"), sem("g_agg_s")
        h_ready, h_done, sq_done, sqa_done = sem("g_h_ready"), sem("g_h_s"), sem("g_sq_s"), sem("g_sqa_s")
        ss_ready, root_done, rs_done, diag_done = sem("g_ss"), sem("g_root_s"), sem("g_rs_s"), sem("g_diag_s")
        rb_ready, v_done, silu_done = sem("g_rb"), sem("g_v_s"), sem("g_silu")
        y_ready, x1_done, stat_done = sem("g_y"), sem("g_x1_s"), sem("g_stat_s")
        stats_taken = sem("g_stats_taken")
        x1_out = [sem("g_out0"), sem("g_out1")]
        ps_ss = ps_a[:, G - 1].rearrange("p a b -> p (a b)")
        ps_rb = ps_t[:, 0].rearrange("p m n q -> p (m n q)")
        xv = io["x"].rearrange("b n d -> (b n) d").rearrange("(n p) d -> p n d", p=P)
        av = io["adj"].rearrange("b n m -> (b n) m").rearrange("(n p) m -> p n m", p=P)
        ov = s.x1_d.rearrange("(n p) d -> p n d", p=P)
        RS_STEPS = 6

        def is0(i):
            return isinstance(i, int) and i == 0

        with nc.Block() as block:
            @block.sync
            def _(sp):
                sp.dma_start(w1[:], io["L0_gnn_W1"].rearrange("(c p) f -> p c f", p=P)).then_inc(ld_w, 16)
                sp.dma_start(w2[:], io["L0_gnn_W2"].rearrange("(c p) d -> p c d", p=P)).then_inc(ld_w, 16)

                def store(i, par):
                    sp.wait_ge(x1_done, i + 1)
                    sp.dma_start(ov[:, ds(i * TT, TT), :], x1[:, par]).then_inc(x1_out[par], 16)

                def load(i, hh, par):
                    if not early(i):
                        sp.wait_ge(xn_done, (i - 1) * TT)
                        sp.wait_ge(xb_done, i - 1)
                    sp.dma_start(xin[:, par], xv[:, ds(i * TT, TT), :]).then_inc(ld_x[par], 16)
                    if not early(i):
                        sp.wait_ge(t_ready, (i - 1) * G)
                    sp.dma_start(adj[:, par], av[:, ds(i * TT, TT), :]).then_inc(ld_a[par], 16)
                    if not early(i):
                        store(i - 2, par)

                steps(sp, NI, load)
                store(NI - 2, 0)
                store(NI - 1, 1)
                for par in range(2):
                    sp.wait_ge(x1_out[par], 16 * (NI // 2) + 16)

            @block.gpsimd
            def _(pool):
                pool.memset(ones[:], 1.0).then_inc(ones_done, 1)
                b2 = s.b2[:].unsqueeze(1).to_broadcast([P, TT, D])

                def step(i, hh, par):
                    pool.wait_ge(ld_x[par], hh * 16 + 16)
                    if not early(i):
                        pool.wait_ge(x1_done, i - 1)
                    pool.tensor_tensor(xb[:, par], xin[:, par], b2, ALU.add).then_inc(xb_done, 1)
                    for f in range(1, FT):
                        pool.wait_ge(sq_done, i * FT + f + 1)
                        if f == 1:
                            if not is0(i):
                                pool.wait_ge(ss_ready, i)
                            pool.tensor_tensor(sqa[:], sq[:, 0], sq[:, 1], ALU.add).then_inc(sqa_done, 2)
                        else:
                            pool.wait_ge(sqa_done, i * FT + f)
                            pool.tensor_tensor(sqa[:], sqa[:], sq[:, f % 2], ALU.add).then_inc(sqa_done, 1)

                steps(pool, NI, step)

            @block.tensor
            def _(pe):
                pe.wait_ge(ones_done, 1)

                def turn_adj(i, hh, par):
                    pe.wait_ge(ld_a[par], hh * 16 + 16)
                    if not is0(i):
                        pe.wait_ge(diag_in, i * G)
                        pe.wait_ge(side_in, i * G)
                    if not early(i):
                        pe.wait_ge(v_done, (i - 1) * 2)
                    for g in range(G):
                        for m in range(R):
                            for n in range(R):
                                mm = pe.transpose(ps_t[:, g, m, n], adj[:, par, g * R + n, m * P:(m + 1) * P],
                                                  s.ident[:])
                        mm.then_inc(t_ready, 1)

                def aggregate(i, par):
                    pe.wait_ge(xn_done, (i + 1) * TT)
                    for g in range(G):
                        pe.wait_ge(diag_in, i * G + g + 1)
                        pe.wait_ge(side_in, i * G + g + 1)
                        if g == 0 and not is0(i):
                            pe.wait_ge(agg_done, i * G)
                        if g == G - 1 and not is0(i):
                            pe.wait_ge(rs_done, (i - 1) * RS_STEPS + 1)
                        for c in range(DH):
                            for m in range(R):
                                mm = pe.matmul(ps_a[:, g, c], xn[:, par, g * R + m, c * P:(c + 1) * P],
                                               adjT[:, par, g, m].rearrange("p n q -> p (n q)"),
                                               start=(m == 0), stop=(m == R - 1))
                        mm.then_inc(a_ready, 1)

                def hidden(i, par):
                    pe.wait_ge(agg_done, (i + 1) * G)
                    for f in range(FT):
                        if not (is0(i) and f < 2):
                            pe.wait_ge(h_done, i * FT + (f - 1))
                        for c in range(DH):
                            mm = pe.matmul(ps_h[:, f % 2], w1[:, c, f * P:(f + 1) * P], agg[:, par, c],
                                           start=(c == 0), stop=(c == DH - 1))
                        mm.then_inc(h_ready, 1)

                def squares(i):
                    pe.wait_ge(sqa_done, (i + 1) * FT)
                    pe.wait_ge(agg_done, (i + 1) * G)
                    for t in range(TT):
                        mm = pe.matmul(ps_ss[:, t:t + 1], sqa[:, t * P:(t + 1) * P], ones[:, 0:1],
                                       start=True, stop=True)
                    mm.then_inc(ss_ready, 1)

                def spread(i):
                    pe.wait_ge(diag_done, (i + 1) * TT)
                    for t in range(TT):
                        mm = pe.matmul(ps_rb[:, t * P:(t + 1) * P], ones[:], diag[:, t], start=True, stop=True)
                    mm.then_inc(rb_ready, 1)

                def project(i, par):
                    if not is0(i):
                        pe.wait_ge(x1_done, i)
                    pe.wait_ge(silu_done, (i + 1) * FT)
                    for t in range(TT):
                        for f in range(FT):
                            mm = pe.matmul(ps_y[:, t], h[:, par, f, t * P:(t + 1) * P], w2[:, f],
                                           start=(f == 0), stop=(f == FT - 1))
                    mm.then_inc(y_ready, 1)

                pe.wait_ge(ld_w, 32)
                turn_adj(0, 0, 0)
                aggregate(0, 0)

                def step(i, hh, par):
                    last = isinstance(i, int) and i == NI - 1
                    hidden(i, par)
                    if not last:
                        turn_adj(i + 1, hh + par, 1 - par)
                    if not is0(i):
                        project(i - 1, 1 - par)
                    squares(i)
                    if not last:
                        aggregate(i + 1, 1 - par)
                    spread(i)

                steps(pe, NI, step)
                project(NI - 1, 1)

            @block.scalar
            def _(act):
                def sides(i, par):
                    for g in range(G):
                        act.wait_ge(diag_in, i * G + g + 1)
                        if not early(i):
                            act.wait_ge(a_ready, (i - 1) * G)
                        flat_in = ps_t[:, g].rearrange("p m n q -> p (m n) q")
                        flat_out = adjT[:, par, g].rearrange("p m n q -> p (m n) q")
                        act.activation(flat_out[:, 1:3], flat_in[:, 1:3], ACT.Identity).then_inc(side_in, 1)

                def aggregates(i, par):
                    for g in range(G):
                        act.wait_ge(a_ready, i * G + g + 1)
                        if not early(i):
                            act.wait_ge(h_ready, (i - 1) * FT)
                        act.activation(agg[:, par, :, g * N:(g + 1) * N], ps_a[:, g], ACT.Identity)\
                            .then_inc(agg_done, 1)

                sides(0, 0)
                aggregates(0, 0)

                def step(i, hh, par):
                    last = isinstance(i, int) and i == NI - 1
                    for f in range(FT):
                        act.wait_ge(h_done, i * FT + f + 1)
                        if not (is0(i) and f < 2):
                            act.wait_ge(sqa_done, i * FT + f - 1)
                        act.activation(sq[:, f % 2], h[:, par, f], ACT.Square)\
                            .then_inc(sq_done, 1)
                    if not last:
                        sides(i + 1, 1 - par)
                    act.wait_ge(rs_done, i * RS_STEPS + 1)
                    act.activation(root[:], var[:], ACT.Sqrt).then_inc(root_done, 1)
                    if not last:
                        aggregates(i + 1, 1 - par)
                    for f in range(FT):
                        act.wait_ge(v_done, i * 2 + f // (FT // 2) + 1)
                        act.activation(h[:, par, f], h[:, par, f], ACT.Silu, scale=s.rw[:, f:f + 1])\
                            .then_inc(silu_done, 1)

                steps(act, NI, step)

            @block.vector
            def _(dve):
                def normalise(i, hh, par):
                    dve.wait_ge(ld_x[par], hh * 16 + 16)
                    if not early(i):
                        dve.wait_ge(a_ready, (i - 1) * G)
                    for t in range(TT):
                        dve.tensor_scalar(xn[:, par, t], xin[:, par, t], s.mv[:, ds(i * TT + t, 1), 0],
                                          s.rstd[:, ds(i * TT + t, 1)], ALU.subtract, ALU.mult)\
                            .then_inc(xn_done, 1)

                def diagonals(i, par):
                    for g in range(G):
                        dve.wait_ge(t_ready, i * G + g + 1)
                        if not early(i):
                            dve.wait_ge(a_ready, (i - 1) * G)
                        flat_in = ps_t[:, g].rearrange("p m n q -> p (m n) q")
                        flat_out = adjT[:, par, g].rearrange("p m n q -> p (m n) q")
                        dve.scalar_tensor_tensor(flat_out[:, 0:4:3], s.ident[:].unsqueeze(1).to_broadcast([P, 2, P]),
                                                 s.eps[:], flat_in[:, 0:4:3], ALU.mult, ALU.add)\
                            .then_inc(diag_in, 1)

                for par in range(2):
                    dve.sem_inc(x1_out[par], 16)
                normalise(0, 0, 0)
                diagonals(0, 0)

                def finish(i, hh, par):
                    dve.wait_ge(y_ready, i + 1)
                    dve.wait_ge(xb_done, i + 1)
                    dve.wait_ge(x1_out[par], hh * 16 + 16)
                    dve.tensor_tensor(x1[:, par], ps_y[:], xb[:, par], ALU.add).then_inc(x1_done, 1)
                    dve.wait_ge(x1_done, i + 1)
                    if not is0(i):
                        dve.wait_ge(stat_done, i * (2 * TT + 1))
                    for t in range(TT):
                        dve.bn_stats(stat[:, t], x1[:, par, t]).then_inc(stat_done, 1)
                    dve.wait_ge(stat_done, i * (2 * TT + 1) + TT)
                    dve.sem_inc(stats_taken, 1)
                    for t in range(TT):
                        dve.bn_aggr(aggr[:, t], stat[:, t]).then_inc(stat_done, 1)
                    dve.wait_ge(stat_done, i * (2 * TT + 1) + 2 * TT)
                    dve.tensor_copy(s.mv2[:, ds(i * TT, TT), :], aggr[:]).then_inc(stat_done, 1)

                def step(i, hh, par):
                    last = isinstance(i, int) and i == NI - 1
                    for f in range(FT):
                        dve.wait_ge(h_ready, i * FT + f + 1)
                        if not early(i):
                            dve.wait_ge(y_ready, i - 1)
                        dve.tensor_scalar(h[:, par, f], ps_h[:, f % 2], s.b1[:, f:f + 1], None, ALU.add)\
                            .then_inc(h_done, 1)
                    if not last:
                        normalise(i + 1, hh + par, 1 - par)
                        diagonals(i + 1, 1 - par)
                    if not is0(i):
                        finish(i - 1, hh + par - 1, 1 - par)
                    dve.wait_ge(ss_ready, i + 1)
                    at = i * RS_STEPS
                    dve.tensor_scalar(var[:], ps_ss[:, 0:TT], 1.0 / F, RMS_EPS, ALU.mult, ALU.add).then_inc(rs_done, 1)
                    dve.wait_ge(root_done, i + 1)
                    dve.wait_ge(rs_done, at + 1)
                    if not is0(i):
                        dve.wait_ge(diag_done, i * TT)
                    newton_rsqrt(dve, (tmp[:, 0], tmp[:, 1]), rs[:], var[:], root[:], rs_done, at + 1)
                    if not is0(i):
                        dve.wait_ge(rb_ready, i)
                    for t in range(TT):
                        dve.tensor_scalar(diag[:, t], s.ident[:], rs[:, t:t + 1], None, ALU.mult)\
                            .then_inc(diag_done, 1)
                    dve.wait_ge(rb_ready, i + 1)
                    dve.wait_ge(sq_done, (i + 1) * FT)
                    half = FT // 2
                    rb = ps_rb.unsqueeze(1).to_broadcast([P, half, W])
                    for m in range(2):
                        dve.tensor_tensor(h[:, par, m * half:(m + 1) * half], h[:, par, m * half:(m + 1) * half],
                                          rb, ALU.mult).then_inc(v_done, 1)

                steps(dve, NI, step)
                finish(NI - 1, NI // 2 - 1, 1)


def stage_norm(s):
    nc = s.nc
    D, DH = s.D, s.DH
    TT = 4
    W = TT * P
    NI = s.T // W
    with ExitStack() as ctx:
        def sb(name, shape, dt=F32):
            return ctx.enter_context(nc.sbuf_tensor(name, shape, dt))

        def sem(name):
            return ctx.enter_context(nc.semaphore(name))

        root = sb("n_root", [P, s.NT])
        xin = sb("n_x", [P, 2, TT, D])
        xn = sb("n_xn", [P, 2, TT, D + 1])
        dx = sb("n_dx", [P, 2, TT, D])
        xT = sb("n_xT", [P, 2, DH, W])
        part = sb("n_part", [P, 2, PARTS, DH, W], BF16)
        rest = sb("n_rest", [P, 2, DH, W])
        pst = ctx.enter_context(nc.psum_tensor("n_ps", [P, 2, 2, DH, W], F32))
        ld_x = [sem("n_ldx0"), sem("n_ldx1")]
        out = [sem("n_out0"), sem("n_out1")]
        var_done, root_done, pad_done = sem("n_var"), sem("n_root_s"), sem("n_pad")
        xn_done, dx_done, turned = sem("n_xn_s"), sem("n_dx_s"), sem("n_turned")
        hi_done, mid_done, rest_done, lo_done, xT_done = (
            sem("n_hi"), sem("n_mid"), sem("n_rest_s"), sem("n_lo"), sem("n_xT_s"))
        xv = s.x1_d.rearrange("(n p) d -> p n d", p=P)
        NOUT = 1 + PARTS

        with nc.Block() as block:
            @block.sync
            def _(sp):
                def store(i, par):
                    sp.wait_ge(lo_done, i + 1)
                    sp.wait_ge(xT_done, i + 1)
                    sp.dma_start(s.xT_d.rearrange("(c p) t -> p c t", p=P)[:, :, ds(i * W, W)], xT[:, par])\
                        .then_inc(out[par], 16)
                    for m in range(PARTS):
                        sp.dma_start(s.dxs_d[m].rearrange("(c p) t -> p c t", p=P)[:, :, ds(i * W, W)],
                                     part[:, par, m]).then_inc(out[par], 16)

                def load(i, h, par):
                    if not early(i):
                        sp.wait_ge(xn_done, (i - 1) * TT)
                    sp.dma_start(xin[:, par], xv[:, ds(i * TT, TT), :]).then_inc(ld_x[par], 16)
                    if not (isinstance(i, int) and i == 0):
                        store(i - 1, 1 - par)

                steps(sp, NI, load)
                store(NI - 1, 1)
                for par in range(2):
                    sp.wait_ge(out[par], 16 * NOUT * (NI // 2))

            @block.gpsimd
            def _(pool):
                for par in range(2):
                    pool.memset(xn[:, par, :, D:D + 1], 0.0).then_inc(pad_done, 1)
                pool.wait_ge(pad_done, 2)

                def step(i, h, par):
                    pool.wait_ge(xn_done, (i + 1) * TT)
                    if not early(i):
                        pool.wait_ge(turned, (i - 1) * 2)
                    pool.tensor_tensor(dx[:, par], xn[:, par, :, 0:D], xn[:, par, :, 1:D + 1], ALU.subtract)\
                        .then_inc(dx_done, 1)

                steps(pool, NI, step)

            @block.tensor
            def _(pe):
                def step(i, h, par):
                    for k in range(2):
                        if k == 0:
                            pe.wait_ge(xn_done, (i + 1) * TT)
                        else:
                            pe.wait_ge(dx_done, i + 1)
                        if not early(i):
                            pe.wait_ge(xT_done, i - 1)
                            pe.wait_ge(rest_done, i - 1)
                        src = xn if k == 0 else dx
                        for t in range(TT):
                            for c in range(DH):
                                mm = pe.transpose(pst[:, par, k, c, t * P:(t + 1) * P],
                                                  src[:, par, t, c * P:(c + 1) * P], s.ident[:])
                        mm.then_inc(turned, 1)

                steps(pe, NI, step)

            @block.scalar
            def _(act):
                act.wait_ge(var_done, 1)
                act.activation(root[:], s.nt[:, 0], ACT.Sqrt).then_inc(root_done, 1)

                def step(i, h, par):
                    act.wait_ge(turned, i * 2 + 1)
                    if not early(i):
                        act.wait_ge(out[par], h * (16 * NOUT))
                    act.activation(xT[:, par], pst[:, par, 0], ACT.Identity).then_inc(xT_done, 1)
                    act.wait_ge(turned, i * 2 + 2)
                    act.activation(part[:, par, 0], pst[:, par, 1], ACT.Identity).then_inc(hi_done, 1)
                    act.wait_ge(rest_done, i + 1)
                    act.activation(part[:, par, 1], rest[:, par], ACT.Identity).then_inc(mid_done, 1)

                steps(act, NI, step)

            @block.vector
            def _(dve):
                dve.tensor_scalar(s.nt[:, 0], s.mv2[:, :, 1], LN_EPS, None, ALU.add).then_inc(var_done, 1)
                dve.wait_ge(root_done, 1)
                dve.wait_ge(var_done, 1)
                newton_rsqrt(dve, (s.nt[:, 1], root[:]), s.rstd[:], s.nt[:, 0], root[:], var_done, 1)

                def normalise(i, h, par):
                    dve.wait_ge(ld_x[par], h * 16 + 16)
                    if not early(i):
                        dve.wait_ge(turned, (i - 1) * 2)
                        dve.wait_ge(dx_done, i - 1)
                    for t in range(TT):
                        dve.tensor_scalar(xn[:, par, t, 0:D], xin[:, par, t], s.mv2[:, ds(i * TT + t, 1), 0],
                                          s.rstd[:, ds(i * TT + t, 1)], ALU.subtract, ALU.mult)\
                            .then_inc(xn_done, 1)

                normalise(0, 0, 0)

                def step(i, h, par):
                    if not (isinstance(i, int) and i == NI - 1):
                        normalise(i + 1, h + par, 1 - par)
                    dve.wait_ge(hi_done, i + 1)
                    if not early(i):
                        dve.wait_ge(lo_done, i - 1)
                    dve.tensor_tensor(rest[:, par], pst[:, par, 1], part[:, par, 0], ALU.subtract).then_inc(rest_done, 1)
                    dve.wait_ge(mid_done, i + 1)
                    dve.wait_ge(rest_done, i + 1)
                    dve.tensor_tensor(part[:, par, 2], rest[:, par], part[:, par, 1], ALU.subtract).then_inc(lo_done, 1)

                steps(dve, NI, step)


def stage_tropical(s):
    nc, io = s.nc, s.io
    D, F, FT = s.D, s.F, s.FT
    NU = D // UNIT
    HALF = 2048
    W = 2 * HALF
    NS = s.T // W
    BANK = 512
    PAIRS, CH = s.PAIRS, s.CH
    VF = FT - 1
    HU = UNIT // 2
    XR = 4
    X_IN = PARTS * 16
    with ExitStack() as ctx:
        def sb(name, shape, dt=F32):
            return ctx.enter_context(nc.sbuf_tensor(name, shape, dt))

        def sem(name):
            return ctx.enter_context(nc.semaphore(name))

        dxs = sb("t_dxs", [P, NU, W], BF16)
        stat = [sb(f"t_stat{g}", [P, UNIT, P], BF16) for g in range(2)]
        row = sb("t_row", [P, XR, HALF])
        run = sb("t_run", [P, VF, HALF])
        aout = [sb(f"t_aout{g}", [P, HALF]) for g in range(2)]
        chain = [ctx.enter_context(nc.psum_tensor(f"t_chain{g}", [P, HALF], F32)) for g in range(2)]

        const_in, pad_done = sem("t_const"), sem("t_pad")
        x_in, w_in = sem("t_x_in"), [sem("t_w_in0"), sem("t_w_in1")]
        row_in = [sem(f"t_row_in{r}") for r in range(XR)]
        summed = sem("t_summed")
        relued = sem("t_relued")
        maxed = sem("t_maxed")
        a_out = [sem("t_a_out0"), sem("t_a_out1")]
        v_out = [sem(f"t_v_out{f}") for f in range(VF)]

        def sums_before(st, c, u):
            return st * (CH * D * 2) + c * (D * 2) + u * (UNIT * 2)

        with nc.Block() as block:
            @block.sync
            def _(sp):
                for g in range(2):
                    sp.dma_start(stat[g][0:SEL], io["sel"]).then_inc(const_in, 16)
                for m in range(PARTS):
                    sp.dma_start(dxs[m * UNIT:(m + 1) * UNIT],
                                 s.dxs_d[m, :, 0:W].rearrange("(u j) t -> j u t", j=UNIT)).then_inc(x_in, 16)

                def load_row(st, d, r):
                    sp.dma_start(row[:, r], s.xT_d[d, ds(st * W + HALF, HALF)].partition_broadcast(P))\
                        .then_inc(row_in[r], 16)

                def reload_row(st, d, r):
                    sp.wait_ge(maxed, st * (D * VF) + (d - (XR - 2)) * VF)
                    load_row(st, d, r)

                for r in range(XR - 1):
                    load_row(0, r, r)

                def step(st, more):
                    reload_row(st, XR - 1, XR - 1)
                    with sp.Fori(1, D // XR) as q:
                        for r in range(XR):
                            reload_row(st, q * XR + r, r)
                    if more:
                        for r in range(XR - 1):
                            sp.wait_ge(maxed, st * (D * VF) + (D + r - (XR - 2)) * VF)
                            load_row(st + 1, r, r)
                    for f in range(VF):
                        sp.wait_ge(maxed, st * (D * VF) + (D * VF + f + 1))
                        sp.dma_start(s.t_d[f * P:(f + 1) * P, ds(st * W + HALF, HALF)], run[:, f]).then_inc(v_out[f], 16)

                with sp.Fori(0, NS - 1) as st:
                    step(st, True)
                step(NS - 1, False)
                for f in range(VF):
                    sp.wait_ge(v_out[f], 16 + NS * 16)

            @block.gpsimd
            def _(pool):
                pool.memset(dxs[SEL:P], 0.0).then_inc(pad_done, 1)
                for g in range(2):
                    pool.memset(stat[g][SEL:P], 0.0).then_inc(pad_done, 1)
                pool.wait_ge(pad_done, 1)
                pool.memset(dxs[SEL:ROWS], 1.0).then_inc(pad_done, 1)

            @block.tensor
            def _(pe):
                pe.wait_ge(const_in, 32)
                pe.wait_ge(pad_done, 4)

                def unit(st, c, u, last):
                    n0 = pe.snap(sums_before(st, c, u))
                    w0 = pe.snap(st * (CH * NU * 32) + c * (NU * 32) + u * 32 + 32)
                    first = isinstance(u, int)
                    for j in range(UNIT):
                        if first and j == 0 and not last:
                            pe.wait_ge(x_in, st * (NU * X_IN) + X_IN)
                        if j % HU == 0:
                            pe.wait_ge(w_in[j // HU], w0)
                        for g in range(2):
                            pe.wait_ge(relued, n0 + (2 * j + g + 1))
                            banks = HALF // BANK // (2 if last else 1)
                            for n in range(banks):
                                lo = (HALF + g * (HALF // 2) if last else 0) + n * BANK
                                mm = pe.matmul(chain[g][:, n * BANK:(n + 1) * BANK], stat[g][:, j, :],
                                               dxs[:, u, lo:lo + BANK],
                                               start=(first and j == 0), stop=True, skip_group_check=True)
                            mm.then_inc(summed, 1)

                with pe.Fori(0, NS) as st:
                    with pe.Fori(0, PAIRS) as c:
                        unit(st, c, 0, False)
                        with pe.Fori(1, NU) as u:
                            unit(st, c, u, False)
                    unit(st, PAIRS, 0, True)
                    with pe.Fori(1, NU) as u:
                        unit(st, PAIRS, u, True)

            @block.scalar
            def _(act):
                act.sem_inc(relued, 2)
                for g in range(2):
                    act.sem_inc(a_out[g], 16)

                def load_w(c, u, half):
                    for g in range(2):
                        act.dma_start(stat[g][SEL:ROWS, half * HU:(half + 1) * HU, :],
                                      s.ws_d[:, c * 2 + g, ds(u * UNIT + half * HU, HU), :]).then_inc(w_in[half], 16)

                def load_x(st, u):
                    for m in range(PARTS):
                        act.dma_start(dxs[m * UNIT:(m + 1) * UNIT, u, :],
                                      s.dxs_d[m, ds(u * UNIT, UNIT), ds(st * W, W)]).then_inc(x_in, 16)

                act.wait_ge(pad_done, 4)
                load_w(0, 0, 0)

                def unit(st, c, u, last, more=True):
                    n0 = act.snap(sums_before(st, c, u))
                    end = isinstance(u, int) and u == NU - 1
                    w = HALF // 2 if last else HALF
                    for j in range(UNIT):
                        for g in range(2):
                            act.wait_ge(summed, n0 + (2 * j + g + 1))
                            if end and j == UNIT - 1:
                                act.wait_ge(a_out[g], st * (CH * 16) + c * 16 + 16)
                                act.activation(aout[g][:, 0:w], chain[g][:, 0:w], ACT.Identity).then_inc(relued, 1)
                            else:
                                act.activation(chain[g][:, 0:w], chain[g][:, 0:w], ACT.Relu).then_inc(relued, 1)
                        if j == 0:
                            load_w(c, u, 1)
                            if last and more and end:
                                load_x(st + 1, NU - 2)
                        if j == HU and not (end and last and not more):
                            if not end:
                                load_w(c, u + 1, 0)
                            elif not last:
                                load_w(c + 1, 0, 0)
                            else:
                                load_w(0, 0, 0)
                    if end:
                        for g in range(2):
                            act.wait_ge(relued, n0 + (2 * UNIT + g + 1))
                            if last:
                                dst = s.t_d[F - P:F, ds(st * W + (HALF + g * (HALF // 2)), HALF // 2)]
                            else:
                                dst = s.t_d[ds(c * (2 * P) + g * P, P), ds(st * W, HALF)]
                            act.dma_start(dst, aout[g][:, 0:w]).then_inc(a_out[g], 16)
                        if last and more:
                            load_x(st + 1, NU - 1)

                def step(st, more):
                    with act.Fori(0, PAIRS) as c:
                        with act.Fori(0, NU - 1) as u:
                            unit(st, c, u, False)
                        unit(st, c, NU - 1, False)
                    if more:
                        unit_and_room(st)
                    else:
                        with act.Fori(0, NU - 1) as u:
                            unit(st, PAIRS, u, True, more)
                    unit(st, PAIRS, NU - 1, True, more)

                def unit_and_room(st):
                    with act.Fori(0, NU - 2) as u:
                        unit(st, PAIRS, u, True)
                        act.wait_ge(summed, sums_before(st, PAIRS, u + 1))
                        load_x(st + 1, u)
                    unit(st, PAIRS, NU - 2, True)

                with act.Fori(0, NS - 1) as st:
                    step(st, True)
                step(NS - 1, False)
                for g in range(2):
                    act.wait_ge(a_out[g], 16 + NS * CH * 16)

            @block.vector
            def _(dve):
                dve.sem_inc(maxed, VF)
                for f in range(VF):
                    dve.sem_inc(v_out[f], 16)

                def rows(st, q, begin):
                    m0 = dve.snap(st * (D * VF) + q * (XR * VF))
                    seen = dve.snap(st * (D // XR * 16) + q * 16 + 16)
                    for r in range(XR):
                        dve.wait_ge(row_in[r], seen)
                        for f in range(VF):
                            dve.wait_ge(maxed, m0 + (r * VF + f + 1))
                            w = s.wt[:, f, ds(q * XR + r, 1)]
                            if begin and r == 0:
                                dve.wait_ge(v_out[f], st * 16 + 16)
                                ins = dve.tensor_scalar(run[:, f], row[:, r], w, None, ALU.add)
                            else:
                                ins = dve.scalar_tensor_tensor(run[:, f], row[:, r], w, run[:, f], ALU.add, ALU.max)
                            ins.then_inc(maxed, 1)

                with dve.Fori(0, NS) as st:
                    rows(st, 0, True)
                    with dve.Fori(1, D // XR) as q:
                        rows(st, q, False)


def stage_ffn(s):
    nc, io = s.nc, s.io
    D, F, FT, DH, NP = s.D, s.F, s.FT, s.DH, s.NP
    TT = 8
    W = TT * P
    BANK = 512
    NI = s.T // W
    TR = 4
    AR = NP - 1
    Q = 2 * (NP - 1)
    DV = Q + 4
    with ExitStack() as ctx:
        def sb(name, shape, dt=F32):
            return ctx.enter_context(nc.sbuf_tensor(name, shape, dt))

        def ps(name, shape):
            return ctx.enter_context(nc.psum_tensor(name, shape, F32))

        def sem(name):
            return ctx.enter_context(nc.semaphore(name))

        wc, wg = sb("f_wc", [P, DH, F]), sb("f_wg", [P, DH, F])
        wd = sb("f_wd", [P, FT, D])
        xT = sb("f_xT", [P, 2, DH, W])
        x1 = sb("f_x1", [P, 2, TT, D])
        t = sb("f_t", [P, TR, W])
        cl = sb("f_cl", [P, 2, FT, W])
        gate = sb("f_gate", [P, 2, W])
        acc = sb("f_acc", [P, 2, 2, W])
        piece = sb("f_piece", [P, AR, W])
        ps_h = ps("f_ps_h", [P, 2, W])
        ps_o = ps("f_ps_o", [P, TT, D])
        ld_w = sem("f_ld_w")
        ld_xT = [sem("f_ldxT0"), sem("f_ldxT1")]
        ld_x1 = [sem("f_ldx10"), sem("f_ldx11")]
        ld_t = [sem(f"f_ldt{r}") for r in range(TR)]
        h_ready, h_read = sem("f_h_ready"), sem("f_h_read")
        aff_done, alu_done, fused = sem("f_aff"), sem("f_alu"), sem("f_fused")
        o_ready, o_done, bias_done = sem("f_o_ready"), sem("f_o_done"), sem("f_bias")
        out = [sem("f_out0"), sem("f_out1")]
        x1v = s.x1_d.rearrange("(n p) d -> p n d", p=P)
        ov = io["out"].rearrange("b n d -> (b n) d").rearrange("(n p) d -> p n d", p=P)
        xTv = s.xT_d.rearrange("(c p) t -> p c t", p=P)

        def is0(i):
            return isinstance(i, int) and i == 0

        with nc.Block() as block:
            @block.sync
            def _(sp):
                sp.dma_start(wc[:], io["L0_ffn_Wc"].rearrange("(c p) f -> p c f", p=P)).then_inc(ld_w, 16)
                sp.dma_start(wg[:], io["L0_ffn_Wg"].rearrange("(c p) f -> p c f", p=P)).then_inc(ld_w, 16)
                sp.dma_start(wd[:], io["L0_ffn_Wd"].rearrange("(c p) d -> p c d", p=P)).then_inc(ld_w, 16)

                def load_xT(i, h, par):
                    if not early(i):
                        sp.wait_ge(h_ready, (i - 1) * (2 * FT))
                    sp.dma_start(xT[:, par], xTv[:, :, ds(i * W, W)]).then_inc(ld_xT[par], 16)

                def store(i, par):
                    sp.wait_ge(o_done, i + 1)
                    sp.dma_start(ov[:, ds(i * TT, TT), :], x1[:, par]).then_inc(out[par], 16)

                load_xT(0, 0, 0)

                def step(i, h, par):
                    if not early(i):
                        sp.wait_ge(out[par], h * 16)
                    sp.dma_start(x1[:, par], x1v[:, ds(i * TT, TT), :]).then_inc(ld_x1[par], 16)
                    for f in range(FT):
                        if not (is0(i) and f < TR):
                            sp.wait_ge(aff_done, (i * FT + f - TR + 1) * (2 * NP))
                        sp.dma_start(t[:, f % TR], s.t_d[f * P:(f + 1) * P, ds(i * W, W)]).then_inc(ld_t[f % TR], 16)
                        if f == 0 and not (isinstance(i, int) and i == NI - 1):
                            load_xT(i + 1, h + par, 1 - par)
                    if not is0(i):
                        store(i - 1, 1 - par)

                steps(sp, NI, step)
                store(NI - 1, 1)
                for par in range(2):
                    sp.wait_ge(out[par], 16 * (NI // 2))

            @block.gpsimd
            def _(pool):
                bd = s.bd[:].unsqueeze(1).to_broadcast([P, TT, D])

                def step(i, h, par):
                    pool.wait_ge(ld_x1[par], h * 16 + 16)
                    pool.tensor_tensor(x1[:, par], x1[:, par], bd, ALU.add).then_inc(bias_done, 1)

                steps(pool, NI, step)

            @block.tensor
            def _(pe):
                pe.wait_ge(ld_w, 48)

                def product(n, w, f, par, slot, fresh):
                    if not fresh:
                        pe.wait_ge(h_read, n - 1)
                    for b in range(W // BANK):
                        for c in range(DH):
                            mm = pe.matmul(ps_h[:, slot, b * BANK:(b + 1) * BANK], w[:, c, f * P:(f + 1) * P],
                                           xT[:, par, c, b * BANK:(b + 1) * BANK], start=(c == 0), stop=(c == DH - 1))
                    mm.then_inc(h_ready, 1)

                def down(i, par, k):
                    if k == 0:
                        pe.wait_ge(fused, (i + 1) * FT)
                        if not is0(i):
                            pe.wait_ge(o_done, i)
                    for f in range(FT):
                        mm = pe.matmul(ps_o[:, k], cl[:, par, f, k * P:(k + 1) * P], wd[:, f],
                                       start=(f == 0), stop=(f == FT - 1))
                    if k == TT - 1:
                        mm.then_inc(o_ready, 1)

                def step(i, h, par):
                    pe.wait_ge(ld_xT[par], h * 16 + 16)
                    for f in range(FT):
                        product(i * (2 * FT) + f, wc, f, par, f % 2, is0(i) and f < 2)
                    for f in range(FT):
                        product(i * (2 * FT) + (FT + f), wg, f, par, f % 2, False)
                        if not is0(i):
                            down(i - 1, 1 - par, f)

                steps(pe, NI, step)
                for k in range(TT):
                    down(NI - 1, 1, k)

            @block.scalar
            def _(act):
                def step(i, h, par):
                    for f in range(FT):
                        act.wait_ge(h_ready, i * (2 * FT) + f + 1)
                        if f == 0 and not early(i):
                            act.wait_ge(o_ready, i - 1)
                        act.activation(cl[:, par, f], ps_h[:, f % 2], ACT.Gelu, bias=s.bc[:, f:f + 1])\
                            .then_inc(h_read, 1)
                    for f in range(FT):
                        n = i * FT + f
                        act.wait_ge(h_ready, i * (2 * FT) + (FT + f + 1))
                        if not (is0(i) and f < 2):
                            act.wait_ge(fused, n - 1)
                        act.activation(gate[:, f % 2], ps_h[:, f % 2], ACT.Sigmoid, bias=s.bg[:, f:f + 1])\
                            .then_inc(h_read, 1)
                        act.wait_ge(ld_t[f % TR], i * (FT // TR * 16) + (f // TR * 16 + 16))
                        for p in range(NP):
                            for side in range(2):
                                q = (p - 1) * 2 + side
                                if p == 0:
                                    dst = acc[:, f % 2, side]
                                else:
                                    dst = piece[:, q % AR]
                                    if not (is0(i) and f == 0 and q < AR):
                                        if q < AR:
                                            act.wait_ge(alu_done, (n - 1) * DV + (q + AR + 1))
                                        else:
                                            act.wait_ge(alu_done, n * DV + (q - AR + 1))
                                act.activation(dst, t[:, f % TR], ACT.Identity,
                                               bias=s.coef[:, 2 * side + 1, f, p:p + 1],
                                               scale=s.coef[:, 2 * side, f, p:p + 1]).then_inc(aff_done, 1)

                steps(act, NI, step)

            @block.vector
            def _(dve):
                def step(i, h, par):
                    for f in range(FT):
                        n = i * FT + f
                        a0, d0 = n * (2 * NP), n * DV
                        cvx, ccv = acc[:, f % 2, 0], acc[:, f % 2, 1]
                        for q in range(Q):
                            dve.wait_ge(aff_done, a0 + (2 + q + 1))
                            if q >= 2:
                                dve.wait_ge(alu_done, d0 + (q - 1))
                            a = acc[:, f % 2, q % 2]
                            dve.tensor_tensor(a, a, piece[:, q % AR], ALU.max if q % 2 == 0 else ALU.min)\
                                .then_inc(alu_done, 1)
                        dve.wait_ge(alu_done, d0 + Q)
                        dve.tensor_tensor(cvx, cvx, ccv, ALU.add).then_inc(alu_done, 1)
                        dve.wait_ge(alu_done, d0 + (Q + 1))
                        dve.wait_ge(h_read, i * (2 * FT) + (FT + f + 1))
                        dve.tensor_tensor(cvx, cvx, cl[:, par, f], ALU.subtract).then_inc(alu_done, 1)
                        dve.wait_ge(alu_done, d0 + (Q + 2))
                        dve.tensor_tensor(cvx, cvx, gate[:, f % 2], ALU.mult).then_inc(alu_done, 1)
                        dve.wait_ge(alu_done, d0 + (Q + 3))
                        dve.tensor_tensor(cl[:, par, f], cl[:, par, f], cvx, ALU.add).then_inc(alu_done, 1)
                        dve.wait_ge(alu_done, d0 + (Q + 4))
                        dve.sem_inc(fused, 1)
                    if not is0(i):
                        finish(i - 1, 1 - par)

                def finish(i, par):
                    dve.wait_ge(o_ready, i + 1)
                    dve.wait_ge(bias_done, i + 1)
                    dve.tensor_tensor(x1[:, par], ps_o[:], x1[:, par], ALU.add).then_inc(o_done, 1)

                steps(dve, NI, step)
                finish(NI - 1, 1)


def build(nc, io):
    with ExitStack() as ctx:
        s = Shared(nc, ctx, io)
        stage_prepare(s)
        stage_gnn(s)
        stage_norm(s)
        stage_tropical(s)
        stage_ffn(s)


def kernel(**inputs):
    import ml_dtypes
    import numpy as np
    import concourse.bacc as bacc
    from concourse.bass_utils import run_bass_kernel_spmd

    arrays = {name: np.ascontiguousarray(a) for name, a in inputs.items()}
    for name, a in arrays.items():
        if a.ndim == 0:
            arrays[name] = a.reshape(1)
    arrays["ident"] = np.eye(P, dtype=np.float32)
    arrays["sel"] = np.ascontiguousarray(np.broadcast_to(
        np.tile(np.eye(UNIT), (PARTS, 1))[:, :, None], (SEL, UNIT, P))).astype(ml_dtypes.bfloat16)
    nc = bacc.Bacc("TRN2", target_bir_lowering=False, num_devices=1)
    io = {name: nc.dram_tensor(f"in_{name}", a.shape, mybir.dt.from_np(a.dtype), kind="ExternalInput").ap()
          for name, a in arrays.items()}
    io["out"] = nc.dram_tensor("out_x", arrays["x"].shape, F32, kind="ExternalOutput").ap()
    build(nc, io)
    r = run_bass_kernel_spmd(nc, [{f"in_{name}": a for name, a in arrays.items()}], core_ids=[0])
    return r.results[0]["out_x"]
```

```python
from contextlib import ExitStack

import concourse.bass as bass
from concourse import mybir

P = 128
F32 = mybir.dt.float32
BF16 = mybir.dt.bfloat16
ALU = mybir.AluOpType
ACT = mybir.ActivationFunctionType
ds = bass.ds

LN_EPS = 1e-5
RMS_EPS = 1e-6
UNIT = 32
PARTS = 3
SEL = PARTS * UNIT
ROWS = SEL + PARTS


def steps(eng, n, body):
    body(0, 0, 0)
    body(1, 0, 1)
    if n > 4:
        with eng.Fori(1, n // 2 - 1) as h:
            body(h * 2, h, 0)
            body(h * 2 + 1, h, 1)
    body(n - 2, n // 2 - 1, 0)
    body(n - 1, n // 2 - 1, 1)


def early(i):
    return isinstance(i, int) and i < 2


class Shared:

    def __init__(self, nc, ctx, io):
        self.nc, self.io = nc, io
        self.B, self.N, self.D = io["x"].shape
        self.F = io["L0_gnn_W1"].shape[1]
        self.T = self.B * self.N
        self.FT, self.DH = self.F // P, self.D // P
        self.NT = self.T // P
        self.NP = io["L0_ffn_sl_cvx"].shape[1]

        def sb(name, shape, dt=F32):
            return ctx.enter_context(nc.sbuf_tensor(name, shape, dt))

        def dram(name, shape, dt=F32):
            return nc.dram_tensor(name, shape, dt, kind="Internal").ap()

        T, D, F, FT, NT, NP = self.T, self.D, self.F, self.FT, self.NT, self.NP
        self.x1_d = dram("x1_scratch", [T, D])
        self.xT_d = dram("xT_scratch", [D, T])
        self.dxs_d = dram("dxs_scratch", [PARTS, D, T], BF16)
        self.PAIRS = FT // 2
        self.CH = self.PAIRS + 1
        self.ws_d = dram("ws_scratch", [PARTS, self.CH * 2, D, P], BF16)
        self.t_d = dram("t_scratch", [F, T])
        self.ident = sb("ident", [P, P])
        self.wt = sb("wt", [P, FT, D + 1])
        self.b1, self.rw, self.bc, self.bg, self.bt, self.al = (
            sb(n, [P, FT]) for n in ("b1", "rw", "bc", "bg", "bt", "al"))
        self.eps = sb("eps", [P, 1])
        self.coef = sb("coef", [P, 4, FT, NP])
        self.b2, self.bd = sb("b2", [P, D]), sb("bd", [P, D])
        self.mv = sb("mv", [P, NT, 2])
        self.rstd = sb("rstd", [P, NT])
        self.nt = sb("newton", [P, 2, NT])


def newton_rsqrt(dve, sh, n, var, root, done, at):
    y, z = sh
    dve.reciprocal(y, root).then_inc(done, 1)
    dve.wait_ge(done, at + 1)
    dve.tensor_tensor(z, y, y, ALU.mult).then_inc(done, 1)
    dve.wait_ge(done, at + 2)
    dve.tensor_tensor(z, z, var, ALU.mult).then_inc(done, 1)
    dve.wait_ge(done, at + 3)
    dve.tensor_scalar(z, z, -0.5, 1.5, ALU.mult, ALU.add).then_inc(done, 1)
    dve.wait_ge(done, at + 4)
    dve.tensor_tensor(n, y, z, ALU.mult).then_inc(done, 1)
    dve.wait_ge(done, at + 5)
    return at + 5


def stage_prepare(s):
    nc, io = s.nc, s.io
    D, F, FT, DH = s.D, s.F, s.FT, s.DH
    with ExitStack() as ctx:
        def sb(name, shape, dt=F32):
            return ctx.enter_context(nc.sbuf_tensor(name, shape, dt))

        def sem(name):
            return ctx.enter_context(nc.semaphore(name))

        dwf = sb("p_dw", [P, FT, D])
        part = sb("p_part", [P, PARTS, DH, F], BF16)
        rest = sb("p_rest", [P, DH, F])
        sig = sb("p_sig", [P, 2, FT])
        psw = ctx.enter_context(nc.psum_tensor("p_psw", [P, DH, F], F32))
        ld, ldw = sem("p_ld"), sem("p_ldw")
        w_done, turned, part_done, rest_done = sem("p_w"), sem("p_turned"), sem("p_part_s"), sem("p_rest_s")
        sig_done, coef_done, ws_out = sem("p_sig_s"), sem("p_coef_s"), sem("p_ws_out")
        NLOAD = 14

        with nc.Block() as block:
            @block.sync
            def _(sp):
                sp.dma_start(s.wt[:, :, 0:D], io["L0_ffn_Wt"].rearrange("(c p) d -> p c d", p=P)).then_inc(ldw, 16)
                sp.dma_start(s.ident[:], io["ident"]).then_inc(ldw, 16)
                with nc.allow_non_contiguous_dma("vectors of f, one value a partition"):
                    sp.dma_start(s.bt[:], io["L0_ffn_bt"].rearrange("(c p) -> p c", p=P)).then_inc(ldw, 16)
                    for dst, name in ((s.b1, "L0_gnn_b1"), (s.rw, "L0_gnn_rms_weight"), (s.bc, "L0_ffn_bc"),
                                      (s.bg, "L0_ffn_bg"), (s.al, "L0_ffn_alpha")):
                        sp.dma_start(dst[:], io[name].rearrange("(c p) -> p c", p=P)).then_inc(ld, 16)
                for n, name in enumerate(("sl_cvx", "of_cvx", "sl_ccv", "of_ccv")):
                    sp.dma_start(s.coef[:, n], io[f"L0_ffn_{name}"].rearrange("(c p) n -> p c n", p=P)).then_inc(ld, 16)
                sp.dma_start(s.b2[:], io["L0_gnn_b2"].partition_broadcast(P)).then_inc(ld, 16)
                sp.dma_start(s.bd[:], io["L0_ffn_bd"].partition_broadcast(P)).then_inc(ld, 16)
                sp.dma_start(s.eps[:], io["L0_gnn_epsilon"].partition_broadcast(P)).then_inc(ld, 16)

                sp.wait_ge(part_done, 3)
                for m in range(PARTS):
                    for c in range(DH):
                        rows = slice(c * P, (c + 1) * P)
                        sp.dma_start(s.ws_d[m, 0:FT, rows, :].rearrange("n p f -> p n f"),
                                     part[:, m, c].rearrange("p (n f) -> p n f", f=P)).then_inc(ws_out, 16)
                        for g in range(2):
                            sp.dma_start(s.ws_d[m, FT + g, rows, :], part[:, m, c, F - P:F]).then_inc(ws_out, 16)
                sp.wait_ge(ws_out, 16 * PARTS * DH * 3)

            @block.gpsimd
            def _(pool):
                pool.memset(s.wt[:, :, D:D + 1], 0.0).then_inc(w_done, 1)

            @block.tensor
            def _(pe):
                pe.wait_ge(w_done, 1 + FT + 1)
                for c in range(DH):
                    for f in range(FT):
                        mm = pe.transpose(psw[:, c, f * P:(f + 1) * P], dwf[:, f, c * P:(c + 1) * P], s.ident[:])
                mm.then_inc(turned, 1)

            @block.scalar
            def _(act):
                act.wait_ge(turned, 1)
                act.activation(part[:, 0], psw[:], ACT.Identity).then_inc(part_done, 1)
                act.wait_ge(rest_done, 1)
                act.activation(part[:, 1], rest[:], ACT.Identity).then_inc(part_done, 1)
                act.wait_ge(ld, 16 * (NLOAD - 2))
                act.activation(sig[:, 0], s.al[:], ACT.Sigmoid).then_inc(sig_done, 1)
                act.wait_ge(ld, 16 * (NLOAD - 2))
                act.activation(sig[:, 1], s.al[:], ACT.Sigmoid, scale=-1.0).then_inc(sig_done, 1)

            @block.vector
            def _(dve):
                dve.wait_ge(ldw, 48)
                dve.wait_ge(w_done, 1)
                for f in range(FT):
                    dve.tensor_scalar(s.wt[:, f, 0:D], s.wt[:, f, 0:D], s.bt[:, f:f + 1], None,
                                      ALU.add).then_inc(w_done, 1)
                dve.wait_ge(w_done, 1 + FT)
                dve.tensor_tensor(dwf[:], s.wt[:, :, 0:D], s.wt[:, :, 1:D + 1], ALU.subtract).then_inc(w_done, 1)
                dve.wait_ge(part_done, 1)
                dve.tensor_tensor(rest[:], psw[:], part[:, 0], ALU.subtract).then_inc(rest_done, 1)
                dve.wait_ge(part_done, 2)
                dve.wait_ge(rest_done, 1)
                dve.tensor_tensor(part[:, 2], rest[:], part[:, 1], ALU.subtract).then_inc(part_done, 1)

                dve.wait_ge(sig_done, 2)
                for n in range(4):
                    for f in range(FT):
                        dve.tensor_scalar(s.coef[:, n, f], s.coef[:, n, f], sig[:, n // 2, f:f + 1], None,
                                          ALU.mult).then_inc(coef_done, 1)


def stage_gnn(s):
    nc, io = s.nc, s.io
    D, F, FT, DH, N = s.D, s.F, s.FT, s.DH, s.N
    G = 2
    R = N // P
    TT = G * R
    W = TT * P
    NI = s.T // W
    with ExitStack() as ctx:
        def sb(name, shape, dt=F32):
            return ctx.enter_context(nc.sbuf_tensor(name, shape, dt))

        def ps(name, shape):
            return ctx.enter_context(nc.psum_tensor(name, shape, F32))

        def sem(name):
            return ctx.enter_context(nc.semaphore(name))

        w1 = sb("g_w1", [P, DH, F])
        w2 = sb("g_w2", [P, FT, D])
        ones = sb("g_ones", [P, P])
        xin = sb("g_x", [P, 2, TT, D])
        adj = sb("g_adj", [P, 2, TT, N])
        xn = sb("g_xn", [P, 2, TT, D])
        xb = sb("g_xb", [P, 2, TT, D])
        adjT = sb("g_adjT", [P, 2, G, R, R, P])
        agg = sb("g_agg", [P, 2, DH, W])
        h = sb("g_h", [P, 2, FT, W])
        sq = sb("g_sq", [P, 2, W])
        sqa = sb("g_sqa", [P, W])
        var = sb("g_var", [P, W])
        root = sb("g_root", [P, W])
        rs = sb("g_rs", [P, W])
        tmp = sb("g_tmp", [P, 2, W])
        xstat = sb("g_xstat", [P, TT, 6])
        xaggr = sb("g_xaggr", [P, TT, 2])
        xvar = sb("g_xvar", [P, TT])
        xroot = sb("g_xroot", [P, TT])
        xrs = sb("g_xrs", [P, TT])
        xtmp = sb("g_xtmp", [P, 2, TT])
        x1 = sb("g_x1", [P, 2, TT, D])
        stat = sb("g_stat", [P, TT, 6])
        aggr = sb("g_aggr", [P, TT, 2])
        ps_h = ps("g_ps_h", [P, 2, W])
        ps_t = ps("g_ps_t", [P, G, R, R, P])
        ps_a = ps("g_ps_a", [P, G, DH, N])
        ps_y = ps("g_ps_y", [P, TT, D])
        ld_w = sem("g_ld_w")
        ld_x, ld_a = [sem("g_ldx0"), sem("g_ldx1")], [sem("g_lda0"), sem("g_lda1")]
        ones_done, xn_done, xb_done = sem("g_ones_s"), sem("g_xn_s"), sem("g_xb_s")
        t_ready, diag_in, side_in = sem("g_t_ready"), sem("g_diag_in"), sem("g_side_in")
        a_ready, agg_done = sem("g_a_ready"), sem("g_agg_s")
        h_ready, h_done, sq_done, sqa_done = sem("g_h_ready"), sem("g_h_s"), sem("g_sq_s"), sem("g_sqa_s")
        ss_ready, root_done, rs_done = sem("g_ss"), sem("g_root_s"), sem("g_rs_s")
        v_done, silu_done = sem("g_v_s"), sem("g_silu")
        y_ready, x1_done, stat_done = sem("g_y"), sem("g_x1_s"), sem("g_stat_s")
        stats_taken = sem("g_stats_taken")
        xst_done, xst_taken, xroot_done = sem("g_xst"), sem("g_xst_taken"), sem("g_xroot_s")
        x1_out = [sem("g_out0"), sem("g_out1")]
        ps_ss = ps_t[:, 0].rearrange("p m n q -> p (m n q)")
        xv = io["x"].rearrange("b n d -> (b n) d").rearrange("(n p) d -> p n d", p=P)
        av = io["adj"].rearrange("b n m -> (b n) m").rearrange("(n p) m -> p n m", p=P)
        ov = s.x1_d.rearrange("(n p) d -> p n d", p=P)
        XST = 2 * TT + 6
        RS_STEPS = 6

        def is0(i):
            return isinstance(i, int) and i == 0

        with nc.Block() as block:
            @block.sync
            def _(sp):
                def store(i, par):
                    sp.wait_ge(x1_done, i + 1)
                    sp.dma_start(ov[:, ds(i * TT, TT), :], x1[:, par]).then_inc(x1_out[par], 16)

                def load_x(i, par):
                    sp.dma_start(xin[:, par], xv[:, ds(i * TT, TT), :]).then_inc(ld_x[par], 16)

                def load_adj(i, par):
                    sp.dma_start(adj[:, par], av[:, ds(i * TT, TT), :]).then_inc(ld_a[par], 16)

                def step(i, hh, par):
                    if not early(i):
                        store(i - 2, par)
                    if not (isinstance(i, int) and i >= NI - 2):
                        sp.wait_ge(t_ready, (i + 1) * G)
                        load_adj(i + 2, par)
                        sp.wait_ge(xn_done, (i + 1) * TT)
                        sp.wait_ge(xb_done, i + 1)
                        load_x(i + 2, par)

                for par in range(2):
                    load_x(par, par)
                    load_adj(par, par)
                    if par == 0:
                        sp.dma_start(w1[:], io["L0_gnn_W1"].rearrange("(c p) f -> p c f", p=P)).then_inc(ld_w, 16)
                        sp.dma_start(w2[:], io["L0_gnn_W2"].rearrange("(c p) d -> p c d", p=P)).then_inc(ld_w, 16)
                steps(sp, NI, step)
                store(NI - 2, 0)
                store(NI - 1, 1)
                for par in range(2):
                    sp.wait_ge(x1_out[par], 16 * (NI // 2) + 16)

            @block.gpsimd
            def _(pool):
                pool.memset(ones[:], 1.0).then_inc(ones_done, 1)
                b2 = s.b2[:].unsqueeze(1).to_broadcast([P, TT, D])

                def step(i, hh, par):
                    for f in range(1, FT):
                        pool.wait_ge(sq_done, i * FT + f + 1)
                        if f == 1:
                            if not is0(i):
                                pool.wait_ge(ss_ready, i)
                            pool.tensor_tensor(sqa[:], sq[:, 0], sq[:, 1], ALU.add).then_inc(sqa_done, 2)
                        else:
                            pool.wait_ge(sqa_done, i * FT + f)
                            pool.tensor_tensor(sqa[:], sqa[:], sq[:, f % 2], ALU.add).then_inc(sqa_done, 1)
                    pool.wait_ge(ld_x[par], hh * 16 + 16)
                    if not early(i):
                        pool.wait_ge(x1_done, i - 1)
                    pool.tensor_tensor(xb[:, par], xin[:, par], b2, ALU.add).then_inc(xb_done, 1)

                steps(pool, NI, step)

            @block.tensor
            def _(pe):
                pe.wait_ge(ones_done, 1)

                def turn_adj(i, hh, par):
                    pe.wait_ge(ld_a[par], hh * 16 + 16)
                    if not is0(i):
                        pe.wait_ge(diag_in, i * G)
                        pe.wait_ge(side_in, i * G)
                    if not early(i):
                        pe.wait_ge(rs_done, (i - 2) * RS_STEPS + 1)
                    for g in range(G):
                        for m in range(R):
                            for n in range(R):
                                mm = pe.transpose(ps_t[:, g, m, n], adj[:, par, g * R + n, m * P:(m + 1) * P],
                                                  s.ident[:])
                        mm.then_inc(t_ready, 1)

                def aggregate(i, par):
                    pe.wait_ge(xn_done, (i + 1) * TT)
                    for g in range(G):
                        pe.wait_ge(diag_in, i * G + g + 1)
                        pe.wait_ge(side_in, i * G + g + 1)
                        if g == 0 and not is0(i):
                            pe.wait_ge(agg_done, i * G)
                        for c in range(DH):
                            for m in range(R):
                                mm = pe.matmul(ps_a[:, g, c], xn[:, par, g * R + m, c * P:(c + 1) * P],
                                               adjT[:, par, g, m].rearrange("p n q -> p (n q)"),
                                               start=(m == 0), stop=(m == R - 1))
                        mm.then_inc(a_ready, 1)

                def hidden(i, par):
                    pe.wait_ge(agg_done, (i + 1) * G)
                    for f in range(FT):
                        if not (is0(i) and f < 2):
                            pe.wait_ge(h_done, i * FT + (f - 1))
                        for c in range(DH):
                            mm = pe.matmul(ps_h[:, f % 2], w1[:, c, f * P:(f + 1) * P], agg[:, par, c],
                                           start=(c == 0), stop=(c == DH - 1))
                        mm.then_inc(h_ready, 1)

                def squares(i):
                    pe.wait_ge(sqa_done, (i + 1) * FT)
                    if not (isinstance(i, int) and i == NI - 1):
                        pe.wait_ge(diag_in, (i + 1) * G + 1)
                        pe.wait_ge(side_in, (i + 1) * G + 1)
                    pe.matmul(ps_ss, ones[:], sqa[:], start=True, stop=True).then_inc(ss_ready, 1)

                def project(i, par, tiles):
                    if tiles[0] == 0:
                        if not is0(i):
                            pe.wait_ge(x1_done, i)
                        pe.wait_ge(silu_done, (i + 1) * FT)
                    for t in tiles:
                        for f in range(FT):
                            mm = pe.matmul(ps_y[:, t], h[:, par, f, t * P:(t + 1) * P], w2[:, f],
                                           start=(f == 0), stop=(f == FT - 1))
                    if tiles[-1] == TT - 1:
                        mm.then_inc(y_ready, 1)

                turn_adj(0, 0, 0)
                aggregate(0, 0)
                pe.wait_ge(ld_w, 32)

                def step(i, hh, par):
                    last = isinstance(i, int) and i == NI - 1
                    hidden(i, par)
                    if not last:
                        turn_adj(i + 1, hh + par, 1 - par)
                    if not is0(i):
                        project(i - 1, 1 - par, (0,))
                    squares(i)
                    if not is0(i):
                        project(i - 1, 1 - par, range(1, TT - 1))
                    if not last:
                        aggregate(i + 1, 1 - par)
                    if not is0(i):
                        project(i - 1, 1 - par, (TT - 1,))

                steps(pe, NI, step)
                project(NI - 1, 1, range(TT))

            @block.scalar
            def _(act):
                def sides(i, par):
                    for g in range(G):
                        act.wait_ge(diag_in, i * G + g + 1)
                        if not early(i):
                            act.wait_ge(a_ready, (i - 1) * G)
                        flat_in = ps_t[:, g].rearrange("p m n q -> p (m n) q")
                        flat_out = adjT[:, par, g].rearrange("p m n q -> p (m n) q")
                        act.activation(flat_out[:, 1:3], flat_in[:, 1:3], ACT.Identity).then_inc(side_in, 1)

                def aggregates(i, par):
                    for g in range(G):
                        act.wait_ge(a_ready, i * G + g + 1)
                        if not early(i):
                            act.wait_ge(h_ready, (i - 1) * FT)
                        act.activation(agg[:, par, :, g * N:(g + 1) * N], ps_a[:, g], ACT.Identity)\
                            .then_inc(agg_done, 1)

                def x_root(i):
                    act.wait_ge(xst_done, i * XST + (2 * TT + 1))
                    act.activation(xroot[:], xvar[:], ACT.Sqrt).then_inc(xroot_done, 1)

                x_root(0)
                sides(0, 0)
                aggregates(0, 0)

                def step(i, hh, par):
                    last = isinstance(i, int) and i == NI - 1
                    for f in range(FT):
                        act.wait_ge(h_done, i * FT + f + 1)
                        if not (is0(i) and f < 2):
                            act.wait_ge(sqa_done, i * FT + f - 1)
                        act.activation(sq[:, f % 2], h[:, par, f], ACT.Square)\
                            .then_inc(sq_done, 1)
                    if not last:
                        x_root(i + 1)
                        sides(i + 1, 1 - par)
                    act.wait_ge(rs_done, i * RS_STEPS + 1)
                    act.activation(root[:], var[:], ACT.Sqrt).then_inc(root_done, 1)
                    for f in range(FT):
                        if f == FT // 2 and not last:
                            aggregates(i + 1, 1 - par)
                        act.wait_ge(v_done, i * 2 + f // (FT // 2) + 1)
                        act.activation(h[:, par, f], h[:, par, f], ACT.Silu, scale=s.rw[:, f:f + 1])\
                            .then_inc(silu_done, 1)

                steps(act, NI, step)

            @block.vector
            def _(dve):
                def x_stats(i, hh, par, k):
                    if k < TT:
                        if k == 0:
                            dve.wait_ge(ld_x[par], hh * 16 + 16)
                        dve.bn_stats(xstat[:, k], xin[:, par, k]).then_inc(xst_done, 1)
                    elif k == TT:
                        if not is0(i):
                            dve.wait_ge(xn_done, i * TT)
                        dve.wait_ge(xst_done, i * XST + TT)
                        dve.sem_inc(xst_taken, 1)
                        for t in range(TT):
                            dve.bn_aggr(xaggr[:, t], xstat[:, t]).then_inc(xst_done, 1)
                    else:
                        dve.wait_ge(xst_done, i * XST + 2 * TT)
                        dve.tensor_scalar(xvar[:], xaggr[:, :, 1], LN_EPS, None, ALU.add).then_inc(xst_done, 1)

                def normalise(i, hh, par):
                    at = i * XST + (2 * TT + 1)
                    dve.wait_ge(xst_done, at)
                    dve.wait_ge(xroot_done, i + 1)
                    newton_rsqrt(dve, (xtmp[:, 0], xtmp[:, 1]), xrs[:], xvar[:], xroot[:], xst_done, at)
                    if not early(i):
                        dve.wait_ge(a_ready, (i - 1) * G)
                    for t in range(TT):
                        dve.tensor_scalar(xn[:, par, t], xin[:, par, t], xaggr[:, t, 0:1], xrs[:, t:t + 1],
                                          ALU.subtract, ALU.mult)\
                            .then_inc(xn_done, 1)

                def diagonals(i, par):
                    for g in range(G):
                        dve.wait_ge(t_ready, i * G + g + 1)
                        if not early(i):
                            dve.wait_ge(a_ready, (i - 1) * G)
                        flat_in = ps_t[:, g].rearrange("p m n q -> p (m n) q")
                        flat_out = adjT[:, par, g].rearrange("p m n q -> p (m n) q")
                        dve.scalar_tensor_tensor(flat_out[:, 0:4:3], s.ident[:].unsqueeze(1).to_broadcast([P, 2, P]),
                                                 s.eps[:], flat_in[:, 0:4:3], ALU.mult, ALU.add)\
                            .then_inc(diag_in, 1)

                for par in range(2):
                    dve.sem_inc(x1_out[par], 16)
                dve.sem_inc(stat_done, 1)
                for k in range(TT + 2):
                    x_stats(0, 0, 0, k)
                normalise(0, 0, 0)
                diagonals(0, 0)

                def finish(i, hh, par, k):
                    if k == 0:
                        dve.wait_ge(y_ready, i + 1)
                        dve.wait_ge(xb_done, i + 1)
                        dve.wait_ge(x1_out[par], hh * 16 + 16)
                        dve.tensor_tensor(x1[:, par], ps_y[:], xb[:, par], ALU.add).then_inc(x1_done, 1)
                    elif k <= TT:
                        dve.wait_ge(x1_done, i + 1)
                        dve.wait_ge(stat_done, i * (2 * TT + 1) + 1)
                        dve.bn_stats(stat[:, k - 1], x1[:, par, k - 1]).then_inc(stat_done, 1)
                    elif k == TT + 1:
                        dve.wait_ge(stat_done, i * (2 * TT + 1) + TT + 1)
                        dve.sem_inc(stats_taken, 1)
                        for t in range(TT):
                            dve.bn_aggr(aggr[:, t], stat[:, t]).then_inc(stat_done, 1)
                    else:
                        dve.wait_ge(stat_done, i * (2 * TT + 1) + 2 * TT + 1)
                        dve.tensor_copy(s.mv[:, ds(i * TT, TT), :], aggr[:]).then_inc(stat_done, 1)

                FINISH = TT + 3

                def step(i, hh, par):
                    last = isinstance(i, int) and i == NI - 1
                    for f in range(FT):
                        dve.wait_ge(h_ready, i * FT + f + 1)
                        if not early(i):
                            dve.wait_ge(y_ready, i - 1)
                        dve.tensor_scalar(h[:, par, f], ps_h[:, f % 2], s.b1[:, f:f + 1], None, ALU.add)\
                            .then_inc(h_done, 1)
                        if not early(i) and 0 < f <= FINISH:
                            finish(i - 2, hh - 1, par, f - 1)
                        if not last and 2 <= f:
                            x_stats(i + 1, hh + par, 1 - par, f - 2)
                    if not last:
                        diagonals(i + 1, 1 - par)
                        normalise(i + 1, hh + par, 1 - par)
                    dve.wait_ge(ss_ready, i + 1)
                    at = i * RS_STEPS
                    dve.tensor_scalar(var[:], ps_ss, 1.0 / F, RMS_EPS, ALU.mult, ALU.add).then_inc(rs_done, 1)
                    dve.wait_ge(root_done, i + 1)
                    dve.wait_ge(rs_done, at + 1)
                    if not is0(i):
                        dve.wait_ge(v_done, i * 2)
                    newton_rsqrt(dve, (tmp[:, 0], tmp[:, 1]), rs[:], var[:], root[:], rs_done, at + 1)
                    dve.wait_ge(sq_done, (i + 1) * FT)
                    half = FT // 2
                    rb = rs[:].unsqueeze(1).to_broadcast([P, half, W])
                    for m in range(2):
                        dve.tensor_tensor(h[:, par, m * half:(m + 1) * half], h[:, par, m * half:(m + 1) * half],
                                          rb, ALU.mult).then_inc(v_done, 1)

                assert FT > FINISH and FT == TT + 4
                steps(dve, NI, step)
                for i in (NI - 2, NI - 1):
                    for k in range(FINISH):
                        finish(i, i // 2, i % 2, k)


def stage_norm(s):
    nc = s.nc
    D, DH = s.D, s.DH
    TT = 4
    W = TT * P
    NI = s.T // W
    with ExitStack() as ctx:
        def sb(name, shape, dt=F32):
            return ctx.enter_context(nc.sbuf_tensor(name, shape, dt))

        def sem(name):
            return ctx.enter_context(nc.semaphore(name))

        root = sb("n_root", [P, s.NT])
        xin = sb("n_x", [P, 2, TT, D])
        xn = sb("n_xn", [P, 2, TT, D + 1])
        dx = sb("n_dx", [P, 2, TT, D])
        xT = sb("n_xT", [P, 2, DH, W])
        part = sb("n_part", [P, 2, PARTS, DH, W], BF16)
        rest = sb("n_rest", [P, 2, DH, W])
        pst = ctx.enter_context(nc.psum_tensor("n_ps", [P, 2, 2, DH, W], F32))
        ld_x = [sem("n_ldx0"), sem("n_ldx1")]
        out = [sem("n_out0"), sem("n_out1")]
        var_done, root_done, pad_done = sem("n_var"), sem("n_root_s"), sem("n_pad")
        xn_done, dx_done, turned = sem("n_xn_s"), sem("n_dx_s"), sem("n_turned")
        hi_done, mid_done, rest_done, lo_done, xT_done = (
            sem("n_hi"), sem("n_mid"), sem("n_rest_s"), sem("n_lo"), sem("n_xT_s"))
        xv = s.x1_d.rearrange("(n p) d -> p n d", p=P)
        NOUT = 1 + PARTS

        with nc.Block() as block:
            @block.sync
            def _(sp):
                def store(i, par):
                    sp.wait_ge(lo_done, i + 1)
                    sp.wait_ge(xT_done, i + 1)
                    sp.dma_start(s.xT_d.rearrange("(c p) t -> p c t", p=P)[:, :, ds(i * W, W)], xT[:, par])\
                        .then_inc(out[par], 16)
                    for m in range(PARTS):
                        sp.dma_start(s.dxs_d[m].rearrange("(c p) t -> p c t", p=P)[:, :, ds(i * W, W)],
                                     part[:, par, m]).then_inc(out[par], 16)

                def load(i, par):
                    sp.dma_start(xin[:, par], xv[:, ds(i * TT, TT), :]).then_inc(ld_x[par], 16)

                def step(i, h, par):
                    sp.wait_ge(xn_done, (i + 1) * TT)
                    load(i + 2, par)
                    store(i, par)

                load(0, 0)
                load(1, 1)
                steps(sp, NI - 2, step)
                store(NI - 2, 0)
                store(NI - 1, 1)
                for par in range(2):
                    sp.wait_ge(out[par], 16 * NOUT * (NI // 2))

            @block.gpsimd
            def _(pool):
                for par in range(2):
                    pool.memset(xn[:, par, :, D:D + 1], 0.0).then_inc(pad_done, 1)
                pool.wait_ge(pad_done, 2)

                def step(i, h, par):
                    pool.wait_ge(xn_done, (i + 1) * TT)
                    if not early(i):
                        pool.wait_ge(turned, (i - 1) * 2)
                    pool.tensor_tensor(dx[:, par], xn[:, par, :, 0:D], xn[:, par, :, 1:D + 1], ALU.subtract)\
                        .then_inc(dx_done, 1)

                steps(pool, NI, step)

            @block.tensor
            def _(pe):
                def step(i, h, par):
                    for k in range(2):
                        if k == 0:
                            pe.wait_ge(xn_done, (i + 1) * TT)
                        else:
                            pe.wait_ge(dx_done, i + 1)
                        if not early(i):
                            pe.wait_ge(xT_done, i - 1)
                            pe.wait_ge(rest_done, i - 1)
                        src = xn if k == 0 else dx
                        for t in range(TT):
                            for c in range(DH):
                                mm = pe.transpose(pst[:, par, k, c, t * P:(t + 1) * P],
                                                  src[:, par, t, c * P:(c + 1) * P], s.ident[:])
                        mm.then_inc(turned, 1)

                steps(pe, NI, step)

            @block.scalar
            def _(act):
                act.wait_ge(var_done, 1)
                act.activation(root[:], s.nt[:, 0], ACT.Sqrt).then_inc(root_done, 1)

                def step(i, h, par):
                    act.wait_ge(turned, i * 2 + 1)
                    if not early(i):
                        act.wait_ge(out[par], h * (16 * NOUT))
                    act.activation(xT[:, par], pst[:, par, 0], ACT.Identity).then_inc(xT_done, 1)
                    act.wait_ge(turned, i * 2 + 2)
                    act.activation(part[:, par, 0], pst[:, par, 1], ACT.Identity).then_inc(hi_done, 1)
                    act.wait_ge(rest_done, i + 1)
                    act.activation(part[:, par, 1], rest[:, par], ACT.Identity).then_inc(mid_done, 1)

                steps(act, NI, step)

            @block.vector
            def _(dve):
                dve.tensor_scalar(s.nt[:, 0], s.mv[:, :, 1], LN_EPS, None, ALU.add).then_inc(var_done, 1)
                dve.wait_ge(root_done, 1)
                dve.wait_ge(var_done, 1)
                newton_rsqrt(dve, (s.nt[:, 1], root[:]), s.rstd[:], s.nt[:, 0], root[:], var_done, 1)

                def normalise(i, h, par):
                    dve.wait_ge(ld_x[par], h * 16 + 16)
                    if not early(i):
                        dve.wait_ge(turned, (i - 1) * 2)
                        dve.wait_ge(dx_done, i - 1)
                    for t in range(TT):
                        dve.tensor_scalar(xn[:, par, t, 0:D], xin[:, par, t], s.mv[:, ds(i * TT + t, 1), 0],
                                          s.rstd[:, ds(i * TT + t, 1)], ALU.subtract, ALU.mult)\
                            .then_inc(xn_done, 1)

                normalise(0, 0, 0)

                def step(i, h, par):
                    if not (isinstance(i, int) and i == NI - 1):
                        normalise(i + 1, h + par, 1 - par)
                    dve.wait_ge(hi_done, i + 1)
                    if not early(i):
                        dve.wait_ge(lo_done, i - 1)
                    dve.tensor_tensor(rest[:, par], pst[:, par, 1], part[:, par, 0], ALU.subtract).then_inc(rest_done, 1)
                    dve.wait_ge(mid_done, i + 1)
                    dve.wait_ge(rest_done, i + 1)
                    dve.tensor_tensor(part[:, par, 2], rest[:, par], part[:, par, 1], ALU.subtract).then_inc(lo_done, 1)

                steps(dve, NI, step)


def stage_tropical(s):
    nc, io = s.nc, s.io
    D, F, FT = s.D, s.F, s.FT
    NU = D // UNIT
    W = 4096
    AT, VT = 2036, 2060
    NS = s.T // W
    BANK = 512
    PAIRS, CH = s.PAIRS, s.CH
    VF = FT - 1
    HU = UNIT // 2
    XR = 4
    X_IN = PARTS * 16
    with ExitStack() as ctx:
        def sb(name, shape, dt=F32):
            return ctx.enter_context(nc.sbuf_tensor(name, shape, dt))

        def sem(name):
            return ctx.enter_context(nc.semaphore(name))

        dxs = sb("t_dxs", [P, NU, W], BF16)
        stat = [sb(f"t_stat{g}", [P, UNIT, P], BF16) for g in range(2)]
        row = sb("t_row", [P, XR, VT])
        run = sb("t_run", [P, VF, VT])
        aout = [sb(f"t_aout{g}", [P, AT]) for g in range(2)]
        chain = [ctx.enter_context(nc.psum_tensor(f"t_chain{g}", [P, 4 * BANK], F32)) for g in range(2)]

        const_in, pad_done, stat_pad = sem("t_const"), sem("t_pad"), sem("t_stat_pad")
        x0_in, x_in, w_in = sem("t_x0_in"), sem("t_x_in"), [sem("t_w_in0"), sem("t_w_in1")]
        row_in = [sem(f"t_row_in{r}") for r in range(XR)]
        summed = sem("t_summed")
        relued = sem("t_relued")
        maxed = sem("t_maxed")
        a_out = [sem("t_a_out0"), sem("t_a_out1")]
        v_out = [sem(f"t_v_out{f}") for f in range(VF)]

        def sums_before(st, c, u):
            return st * (CH * D * 2) + c * (D * 2) + u * (UNIT * 2)

        with nc.Block() as block:
            @block.sync
            def _(sp):
                for g in range(2):
                    sp.dma_start(stat[g][0:SEL], io["sel"]).then_inc(const_in, 16)
                for m in range(PARTS):
                    sp.dma_start(dxs[m * UNIT:(m + 1) * UNIT, 0], s.dxs_d[m, 0:UNIT, 0:W]).then_inc(x0_in, 16)

                def load_row(st, d, r):
                    sp.dma_start(row[:, r], s.xT_d[d, ds(st * W + AT, VT)].partition_broadcast(P))\
                        .then_inc(row_in[r], 16)

                def reload_row(st, d, r):
                    sp.wait_ge(maxed, st * (D * VF) + (d - (XR - 2)) * VF)
                    load_row(st, d, r)

                for r in range(XR - 1):
                    load_row(0, r, r)
                for m in range(PARTS):
                    sp.dma_start(dxs[m * UNIT:(m + 1) * UNIT, 1:NU],
                                 s.dxs_d[m, UNIT:D, 0:W].rearrange("(u j) t -> j u t", j=UNIT)).then_inc(x_in, 16)

                def step(st, more):
                    reload_row(st, XR - 1, XR - 1)
                    with sp.Fori(1, D // XR) as q:
                        for r in range(XR):
                            reload_row(st, q * XR + r, r)
                    if more:
                        for r in range(XR - 1):
                            sp.wait_ge(maxed, st * (D * VF) + (D + r - (XR - 2)) * VF)
                            load_row(st + 1, r, r)
                    for f in range(VF):
                        sp.wait_ge(maxed, st * (D * VF) + (D * VF + f + 1))
                        sp.dma_start(s.t_d[f * P:(f + 1) * P, ds(st * W + AT, VT)], run[:, f]).then_inc(v_out[f], 16)

                with sp.Fori(0, NS - 1) as st:
                    step(st, True)
                step(NS - 1, False)
                for f in range(VF):
                    sp.wait_ge(v_out[f], 16 + NS * 16)

            @block.gpsimd
            def _(pool):
                for u in range(NU):
                    pool.memset(dxs[SEL:P, u], 0.0).then_inc(pad_done, 1)
                    pool.wait_ge(pad_done, 2 * u + 1)
                    pool.memset(dxs[SEL:ROWS, u], 1.0).then_inc(pad_done, 1)

            @block.tensor
            def _(pe):
                pe.wait_ge(const_in, 32)
                pe.wait_ge(pad_done, 2)

                def unit(st, c, u, last):
                    n0 = pe.snap(sums_before(st, c, u))
                    w0 = pe.snap(st * (CH * NU * 32) + c * (NU * 32) + u * 32 + 32)
                    first = isinstance(u, int)
                    for j in range(UNIT):
                        if j == 0 and not last:
                            if first:
                                pe.wait_ge(x0_in, st * X_IN + X_IN)
                            else:
                                pe.wait_ge(pad_done, 2 * NU)
                                pe.wait_ge(x_in, st * ((NU - 1) * X_IN) + X_IN)
                        if j % HU == 0:
                            pe.wait_ge(w_in[j // HU], w0)
                        for g in range(2):
                            pe.wait_ge(relued, n0 + (2 * j + g + 1))
                            w = VT // 2 if last else AT
                            x0 = AT + g * (VT // 2) if last else 0
                            for lo in range(0, w, BANK):
                                hi = min(lo + BANK, w)
                                mm = pe.matmul(chain[g][:, lo:hi], stat[g][:, j, :], dxs[:, u, x0 + lo:x0 + hi],
                                               start=(first and j == 0), stop=True, skip_group_check=True)
                            mm.then_inc(summed, 1)

                with pe.Fori(0, NS) as st:
                    with pe.Fori(0, PAIRS) as c:
                        unit(st, c, 0, False)
                        with pe.Fori(1, NU) as u:
                            unit(st, c, u, False)
                    unit(st, PAIRS, 0, True)
                    with pe.Fori(1, NU) as u:
                        unit(st, PAIRS, u, True)

            @block.scalar
            def _(act):
                act.sem_inc(relued, 2)
                for g in range(2):
                    act.sem_inc(a_out[g], 16)

                def load_w(c, u, half):
                    for g in range(2):
                        act.dma_start(stat[g][SEL:ROWS, half * HU:(half + 1) * HU, :],
                                      s.ws_d[:, c * 2 + g, ds(u * UNIT + half * HU, HU), :]).then_inc(w_in[half], 16)

                def load_x(st, u):
                    arrived = x0_in if isinstance(u, int) and u == 0 else x_in
                    for m in range(PARTS):
                        act.dma_start(dxs[m * UNIT:(m + 1) * UNIT, u, :],
                                      s.dxs_d[m, ds(u * UNIT, UNIT), ds(st * W, W)]).then_inc(arrived, 16)

                act.wait_ge(stat_pad, 2)
                load_w(0, 0, 0)

                def unit(st, c, u, last, more=True):
                    n0 = act.snap(sums_before(st, c, u))
                    end = isinstance(u, int) and u == NU - 1
                    w = VT // 2 if last else AT
                    for j in range(UNIT):
                        for g in range(2):
                            act.wait_ge(summed, n0 + (2 * j + g + 1))
                            if end and j == UNIT - 1:
                                act.wait_ge(a_out[g], st * (CH * 16) + c * 16 + 16)
                                act.activation(aout[g][:, 0:w], chain[g][:, 0:w], ACT.Identity).then_inc(relued, 1)
                            else:
                                act.activation(chain[g][:, 0:w], chain[g][:, 0:w], ACT.Relu).then_inc(relued, 1)
                        if j == 0:
                            load_w(c, u, 1)
                            if last and more and end:
                                load_x(st + 1, NU - 2)
                        if j == HU and not (end and last and not more):
                            if not end:
                                load_w(c, u + 1, 0)
                            elif not last:
                                load_w(c + 1, 0, 0)
                            else:
                                load_w(0, 0, 0)
                    if end:
                        for g in range(2):
                            act.wait_ge(relued, n0 + (2 * UNIT + g + 1))
                            if last:
                                dst = s.t_d[F - P:F, ds(st * W + (AT + g * (VT // 2)), w)]
                            else:
                                dst = s.t_d[ds(c * (2 * P) + g * P, P), ds(st * W, AT)]
                            act.dma_start(dst, aout[g][:, 0:w]).then_inc(a_out[g], 16)
                        if last and more:
                            load_x(st + 1, NU - 1)

                def step(st, more):
                    with act.Fori(0, PAIRS) as c:
                        with act.Fori(0, NU - 1) as u:
                            unit(st, c, u, False)
                        unit(st, c, NU - 1, False)
                    if more:
                        unit_and_room(st)
                    else:
                        with act.Fori(0, NU - 1) as u:
                            unit(st, PAIRS, u, True, more)
                    unit(st, PAIRS, NU - 1, True, more)

                def unit_and_room(st):
                    unit(st, PAIRS, 0, True)
                    act.wait_ge(summed, sums_before(st, PAIRS, 1))
                    load_x(st + 1, 0)
                    with act.Fori(1, NU - 2) as u:
                        unit(st, PAIRS, u, True)
                        act.wait_ge(summed, sums_before(st, PAIRS, u + 1))
                        load_x(st + 1, u)
                    unit(st, PAIRS, NU - 2, True)

                with act.Fori(0, NS - 1) as st:
                    step(st, True)
                step(NS - 1, False)
                for g in range(2):
                    act.wait_ge(a_out[g], 16 + NS * CH * 16)

            @block.vector
            def _(dve):
                for g in range(2):
                    dve.memset(stat[g][SEL:P], 0.0).then_inc(stat_pad, 1)
                dve.sem_inc(maxed, VF)
                for f in range(VF):
                    dve.sem_inc(v_out[f], 16)

                def rows(st, q, begin):
                    m0 = dve.snap(st * (D * VF) + q * (XR * VF))
                    seen = dve.snap(st * (D // XR * 16) + q * 16 + 16)
                    for r in range(XR):
                        dve.wait_ge(row_in[r], seen)
                        for f in range(VF):
                            dst, src = run[:, f], row[:, r]
                            dve.wait_ge(maxed, m0 + (r * VF + f + 1))
                            w = s.wt[:, f, ds(q * XR + r, 1)]
                            if begin and r == 0:
                                dve.wait_ge(v_out[f], st * 16 + 16)
                                ins = dve.tensor_scalar(dst, src, w, None, ALU.add)
                            else:
                                ins = dve.scalar_tensor_tensor(dst, src, w, dst, ALU.add, ALU.max)
                            ins.then_inc(maxed, 1)

                with dve.Fori(0, NS) as st:
                    rows(st, 0, True)
                    with dve.Fori(1, D // XR) as q:
                        rows(st, q, False)


def stage_ffn(s):
    nc, io = s.nc, s.io
    D, F, FT, DH, NP = s.D, s.F, s.FT, s.DH, s.NP
    TT = 8
    W = TT * P
    BANK = 512
    NI = s.T // W
    TR = 4
    GR = 4
    OT = 2
    OQ = TT // OT
    CHAIN = 3
    X0 = 5
    C0, C1 = 1, 3
    ORDER = ("x_pair", "end_sum", "c_pair", "end_sub", "c_pair2", "end_mul", "c_merge2", "end_add",
             "x_6", "c_4", "x_chain", "c_5", "x_7", "c_6", "c_7")
    DV = len(ORDER)
    ENDS = 4
    POS = {name: k + 1 for k, name in enumerate(ORDER)}
    FIRST = {name: ENDS + k + 1 for k, name in enumerate(x for x in ORDER if x[:4] != "end_")}
    USED = ("x_pair", "c_pair", "c_merge2", "x_6", "c_4", "c_5", "x_7", "c_6", "c_7")
    PIECES = len(USED)
    AR = 6
    DOWN_SLOTS = FT - 2
    DOWN = TT * (FT + 1) // DOWN_SLOTS
    TAKE = {-(-(q + 1) * OT * (FT + 1) // DOWN): q for q in range(OQ)}
    assert (NP, FT % GR, FT % TR, X0 + 3, DOWN * DOWN_SLOTS) == (8, 0, 0, NP, TT * (FT + 1))
    with ExitStack() as ctx:
        def sb(name, shape, dt=F32):
            return ctx.enter_context(nc.sbuf_tensor(name, shape, dt))

        def ps(name, shape):
            return ctx.enter_context(nc.psum_tensor(name, shape, F32))

        def sem(name):
            return ctx.enter_context(nc.semaphore(name))

        wc, wg = sb("f_wc", [P, DH, F]), sb("f_wg", [P, DH, F])
        wd = sb("f_wd", [P, FT, D])
        dif = sb("f_dif", [P, 4, FT, NP - 1])
        rel = sb("f_rel", [P, 2, FT, NP])
        base = sb("f_base", [P, FT])
        diag = sb("f_diag", [P, FT, CHAIN, P])
        xT = sb("f_xT", [P, 2, DH, W])
        x1 = sb("f_x1", [P, TT, D])
        t = sb("f_t", [P, TR, W])
        cl = sb("f_cl", [P, 2, FT, W])
        gate = sb("f_gate", [P, GR, W])
        cvx, ccv = sb("f_cvx", [P, 2, W]), sb("f_ccv", [P, W])
        piece = sb("f_piece", [P, AR, W])
        ps_h = ps("f_ps_h", [P, 2, W])
        ps_o = ps("f_ps_o", [P, 2, OT, D])
        chain = ps("f_chain", [P, W])
        ld_w, ld_wd, tables_done, diag_done = sem("f_ld_w"), sem("f_ld_wd"), sem("f_tables"), sem("f_diag_s")
        ld_xT = [sem("f_ldxT0"), sem("f_ldxT1")]
        ld_x1 = sem("f_ldx1")
        ld_t = [sem(f"f_ldt{r}") for r in range(TR)]
        h_ready, h_read, chain_fresh = sem("f_h_ready"), sem("f_h_read"), sem("f_chain_fresh")
        piece_done, relued, chained, alu_done = sem("f_piece_s"), sem("f_relued"), sem("f_chained"), sem("f_alu")
        o_ready, o_done, out = sem("f_o_ready"), sem("f_o_done"), sem("f_out")
        x1v = s.x1_d.rearrange("(n p) d -> p n d", p=P)
        ov = io["out"].rearrange("b n d -> (b n) d").rearrange("(n p) d -> p n d", p=P)
        xTv = s.xT_d.rearrange("(c p) t -> p c t", p=P)
        AHEAD = 4

        def is0(i):
            return isinstance(i, int) and i == 0

        def is_last(i):
            return isinstance(i, int) and i == NI - 1

        def gelu_read(i, f):
            return i * (2 * FT) + (2 * f + 3 if f % 2 == 0 else 2 * f + 2)

        def done(i, f, name):
            return (i * FT + f) * DV + (FIRST if is0(i) and f == 0 else POS)[name]

        def done_before(i, f, name):
            return done(i, f - 1, name) if f > 0 else done(i - 1, FT - 1, name)

        with nc.Block() as block:
            @block.sync
            def _(sp):
                def load_xT(i, h, par):
                    if not early(i):
                        sp.wait_ge(h_ready, (i - 1) * (2 * FT))
                    sp.dma_start(xT[:, par], xTv[:, :, ds(i * W, W)]).then_inc(ld_xT[par], 16)

                def load_x1(i):
                    if not is0(i):
                        sp.wait_ge(out, i * 16)
                    sp.dma_start(x1[:], x1v[:, ds(i * TT, TT), :]).then_inc(ld_x1, 16)

                def store(i):
                    sp.wait_ge(o_done, (i + 1) * OQ)
                    sp.dma_start(ov[:, ds(i * TT, TT), :], x1[:]).then_inc(out, 16)

                load_xT(0, 0, 0)
                sp.dma_start(wg[:], io["L0_ffn_Wg"].rearrange("(c p) f -> p c f", p=P)).then_inc(ld_w, 16)
                sp.dma_start(wc[:], io["L0_ffn_Wc"].rearrange("(c p) f -> p c f", p=P)).then_inc(ld_w, 16)

                def step(i, h, par):
                    for f in range(FT):
                        if not (is0(i) and f < TR):
                            sp.wait_ge(alu_done, (i * FT + f - TR + 1) * DV)
                        sp.dma_start(t[:, f % TR], s.t_d[f * P:(f + 1) * P, ds(i * W, W)]).then_inc(ld_t[f % TR], 16)
                        if f == 0 and not is_last(i):
                            load_xT(i + 1, h + par, 1 - par)
                        if f == 0 and is0(i):
                            sp.dma_start(wd[:], io["L0_ffn_Wd"].rearrange("(c p) d -> p c d", p=P)).then_inc(ld_wd, 16)
                        if f == 2 and not early(i):
                            store(i - 2)
                        if f == 3 and not is0(i):
                            load_x1(i - 1)

                steps(sp, NI, step)
                store(NI - 2)
                load_x1(NI - 1)
                store(NI - 1)
                sp.wait_ge(out, NI * 16)

            @block.gpsimd
            def _(pool):
                pool.wait_ge(tables_done, 5)
                for f in range(FT):
                    for m in range(CHAIN):
                        slope = dif[:, 0, f, m + 1:m + 2] if m < CHAIN - 1 else s.coef[:, 0, f, CHAIN:CHAIN + 1]
                        pool.tensor_scalar(diag[:, f, m], s.ident[:], slope, None, ALU.mult).then_inc(diag_done, 1)

            @block.tensor
            def _(pe):
                NB = W // BANK

                def product(n, w, f, par, slot, banks=range(NB), fresh=False):
                    if not fresh and banks[0] == 0:
                        pe.wait_ge(h_read, n - 1)
                    for b in banks:
                        for c in range(DH):
                            mm = pe.matmul(ps_h[:, slot, b * BANK:(b + 1) * BANK], w[:, c, f * P:(f + 1) * P],
                                           xT[:, par, c, b * BANK:(b + 1) * BANK], start=(c == 0), stop=(c == DH - 1))
                    if banks[-1] == NB - 1:
                        mm.then_inc(h_ready, 1)

                def product_ahead(i, f, par, k, banks=range(NB)):
                    if is_last(i) and f >= FT - 2:
                        return
                    ahead = f - f % 2 + 2 + k
                    product(i * (2 * FT) + (AHEAD + 2 * f + k), wg if f % 2 == 0 else wc, ahead % FT,
                            par if ahead < FT else 1 - par, k, banks)

                def link(i, f, m):
                    pe.wait_ge(relued, i * (FT * CHAIN) + (f * CHAIN + m + 1))
                    for b in range(W // BANK):
                        mm = pe.matmul(chain[:, b * BANK:(b + 1) * BANK], diag[:, f, m],
                                       t[:, f % TR, b * BANK:(b + 1) * BANK], start=False, stop=True,
                                       skip_group_check=True)
                    mm.then_inc(chained, 1)

                def down(i, par, part, after):
                    if part == 0:
                        pe.wait_ge(alu_done, after)
                    for j in range(part * DOWN, (part + 1) * DOWN):
                        k, f = j // (FT + 1), j % (FT + 1) - 1
                        q = k // OT
                        if k % OT == 0 and f < 0 and not (is0(i) and q < 2):
                            pe.wait_ge(o_done, i * OQ + (q - 1))
                        if f < 0:
                            mm = pe.matmul(ps_o[:, q % 2, k % OT], s.ident[:], s.bd[:], start=True, stop=False)
                        else:
                            mm = pe.matmul(ps_o[:, q % 2, k % OT], cl[:, par, f, k * P:(k + 1) * P], wd[:, f],
                                           start=False, stop=(f == FT - 1))
                        if k % OT == OT - 1 and f == FT - 1:
                            mm.then_inc(o_ready, 1)

                def step(i, h, par):
                    for f in range(FT):
                        if f == FT - 2 and not is_last(i):
                            pe.wait_ge(ld_xT[1 - par], (h + par) * 16 + 16)
                        link(i, f, 0)
                        product_ahead(i, f, par, 0, range(NB // 2))
                        link(i, f, 1)
                        product_ahead(i, f, par, 0, range(NB // 2, NB))
                        link(i, f, 2)
                        product_ahead(i, f, par, 1)
                        if not is0(i) and 1 <= f <= DOWN_SLOTS:
                            down(i - 1, 1 - par, f - 1, done(i, 0, "end_add"))

                pe.wait_ge(ld_xT[0], 16)
                pe.wait_ge(ld_w, 32)
                for b in range(NB):
                    mm = pe.matmul(chain[:, b * BANK:(b + 1) * BANK], s.ident[:], xT[:, 0, 0, b * BANK:(b + 1) * BANK],
                                   start=True, stop=True)
                mm.then_inc(chain_fresh, 1)
                product(0, wg, 0, 0, 0, fresh=True)
                product(1, wg, 1, 0, 1, fresh=True)
                product(2, wc, 0, 0, 0)
                product(3, wc, 1, 0, 1)
                pe.wait_ge(diag_done, FT * CHAIN)
                pe.wait_ge(ld_wd, 16)
                steps(pe, NI, step)
                for part in range(DOWN_SLOTS):
                    down(NI - 1, 1, part, NI * FT * DV + ENDS)

            @block.scalar
            def _(act):
                def gate_of(f, slot):
                    act.activation(gate[:, f % GR], ps_h[:, slot], ACT.Sigmoid, bias=s.bg[:, f:f + 1])\
                        .then_inc(h_read, 1)

                def gelu_of(f, par, slot):
                    act.activation(cl[:, par, f], ps_h[:, slot], ACT.Gelu, bias=s.bc[:, f:f + 1]).then_inc(h_read, 1)

                def product_ahead(i, f, par, k):
                    if is_last(i) and f >= FT - 2:
                        return
                    ahead = f - f % 2 + 2 + k
                    act.wait_ge(h_ready, i * (2 * FT) + (AHEAD + 2 * f + k + 1))
                    if f % 2 == 0:
                        if not (is0(i) and f == 0):
                            act.wait_ge(alu_done, done(i, f, "end_mul") if k == 1 else done_before(i, f, "end_mul"))
                        gate_of(ahead % FT, k)
                    else:
                        if ahead == FT and not is0(i):
                            act.wait_ge(o_ready, i * OQ)
                        gelu_of(ahead % FT, par if ahead < FT else 1 - par, k)

                def step(i, h, par):
                    for f in range(FT):
                        n = i * FT + f
                        ti = t[:, f % TR]

                        def room(k):
                            if k >= AR:
                                act.wait_ge(alu_done, done(i, f, USED[k - AR]))
                            elif not (is0(i) and f == 0):
                                before = max(j for j in range(PIECES) if j % AR == k % AR)
                                act.wait_ge(alu_done, done_before(i, f, USED[before]))

                        def relu(k, side, p):
                            room(k)
                            act.activation(piece[:, k % AR], ti, ACT.Relu, bias=dif[:, 2 * side + 1, f, p:p + 1],
                                           scale=dif[:, 2 * side, f, p:p + 1]).then_inc(piece_done, 1)

                        def line(k, side, p):
                            room(k)
                            act.activation(piece[:, k % AR], ti, ACT.Identity, bias=rel[:, side, f, p:p + 1],
                                           scale=s.coef[:, 2 * side, f, p:p + 1]).then_inc(piece_done, 1)

                        def link(m):
                            act.wait_ge(chained, n * CHAIN + m)
                            act.activation(chain[:], chain[:], ACT.Relu, bias=dif[:, 1, f, m:m + 1])\
                                .then_inc(relued, 1)

                        act.wait_ge(ld_t[f % TR], i * (FT // TR * 16) + (f // TR * 16 + 16))
                        if is0(i) and f == 0:
                            act.wait_ge(chain_fresh, 1)
                        else:
                            act.wait_ge(alu_done, done_before(i, f, "x_chain"))
                        act.activation(chain[:], ti, ACT.Relu, bias=dif[:, 1, f, 0:1], scale=dif[:, 0, f, 0:1])\
                            .then_inc(relued, 1)
                        relu(0, 0, X0 - 1)
                        relu(1, 1, C0 - 1)
                        link(1)
                        relu(2, 1, C1 - 1)
                        line(3, 0, 6)
                        link(2)
                        line(4, 1, 4)
                        product_ahead(i, f, par, 0)
                        line(5, 1, 5)
                        line(6, 0, 7)
                        line(7, 1, 6)
                        product_ahead(i, f, par, 1)
                        line(8, 1, 7)

                act.wait_ge(tables_done, 5)
                for k in range(2):
                    act.wait_ge(h_ready, k + 1)
                    gate_of(k, k)
                for k in range(2):
                    act.wait_ge(h_ready, k + 3)
                    gelu_of(k, 0, k)
                steps(act, NI, step)

            @block.vector
            def _(dve):
                coef = s.coef
                dve.tensor_tensor(dif[:, 0:2], coef[:, 0:2, :, 0:NP - 1], coef[:, 0:2, :, 1:NP], ALU.subtract)\
                    .then_inc(tables_done, 1)
                dve.tensor_tensor(dif[:, 2:4], coef[:, 2:4, :, 1:NP], coef[:, 2:4, :, 0:NP - 1], ALU.subtract)\
                    .then_inc(tables_done, 1)
                for side, p in ((0, X0), (1, C0)):
                    dve.tensor_tensor(rel[:, side], coef[:, 2 * side + 1],
                                      coef[:, 2 * side + 1, :, p:p + 1].to_broadcast([P, FT, NP]), ALU.subtract)\
                        .then_inc(tables_done, 1)
                dve.tensor_tensor(base[:], coef[:, 1, :, X0], coef[:, 3, :, C0], ALU.add).then_inc(tables_done, 1)
                dve.wait_ge(tables_done, 5)

                def end(i, f, par, k, at):
                    x, g = cvx[:, f % 2], cl[:, par, f]
                    dve.wait_ge(alu_done, at)
                    if k == 0:
                        dve.scalar_tensor_tensor(x, x, base[:, f:f + 1], ccv[:], ALU.add, ALU.add)\
                            .then_inc(alu_done, 1)
                    elif k == 1:
                        dve.wait_ge(h_read, gelu_read(i, f))
                        dve.tensor_tensor(x, x, g, ALU.subtract).then_inc(alu_done, 1)
                    elif k == 2:
                        dve.tensor_tensor(x, x, gate[:, f % GR], ALU.mult).then_inc(alu_done, 1)
                    else:
                        dve.tensor_tensor(g, g, x, ALU.add).then_inc(alu_done, 1)

                def step(i, h, par):
                    for f in range(FT):
                        very_first = is0(i) and f == 0
                        ti, x = t[:, f % TR], cvx[:, f % 2]

                        def slope(side, p):
                            return coef[:, 2 * side, f, p:p + 1]

                        def offset(side, p):
                            return rel[:, side, f, p:p + 1]

                        def take(k):
                            dve.wait_ge(piece_done, (i * FT + f) * PIECES + (k + 1))
                            return piece[:, k % AR]

                        def after(name):
                            dve.wait_ge(alu_done, done(i, f, name))

                        def end_before(k):
                            if not very_first:
                                at = (i * FT + f) * DV + 2 * k
                                if f > 0:
                                    end(i, f - 1, par, k, at)
                                else:
                                    end(i - 1, FT - 1, 1 - par, k, at)

                        if not very_first:
                            dve.wait_ge(alu_done, (i * FT + f) * DV - 2)
                        dve.scalar_tensor_tensor(x, ti, slope(0, X0), take(0), ALU.mult, ALU.add)\
                            .then_inc(alu_done, 1)
                        end_before(0)
                        if not very_first:
                            after("end_sum")
                        dve.scalar_tensor_tensor(ccv[:], ti, slope(1, C0), take(1), ALU.mult, ALU.subtract)\
                            .then_inc(alu_done, 1)
                        end_before(1)
                        pair = take(2)
                        dve.scalar_tensor_tensor(pair, ti, slope(1, C1), pair, ALU.mult, ALU.subtract)\
                            .then_inc(alu_done, 1)
                        end_before(2)
                        after("c_pair2")
                        dve.scalar_tensor_tensor(ccv[:], pair, offset(1, C1), ccv[:], ALU.add, ALU.min)\
                            .then_inc(alu_done, 1)
                        end_before(3)
                        dve.tensor_tensor(x, x, take(3), ALU.max).then_inc(alu_done, 1)
                        after("c_merge2")
                        dve.tensor_tensor(ccv[:], ccv[:], take(4), ALU.min).then_inc(alu_done, 1)
                        after("x_6")
                        dve.wait_ge(chained, (i * FT + f + 1) * CHAIN)
                        dve.scalar_tensor_tensor(x, chain[:], offset(0, CHAIN), x, ALU.add, ALU.max)\
                            .then_inc(alu_done, 1)
                        after("c_4")
                        dve.tensor_tensor(ccv[:], ccv[:], take(5), ALU.min).then_inc(alu_done, 1)
                        after("x_chain")
                        dve.tensor_tensor(x, x, take(6), ALU.max).then_inc(alu_done, 1)
                        after("c_5")
                        dve.tensor_tensor(ccv[:], ccv[:], take(7), ALU.min).then_inc(alu_done, 1)
                        after("c_6")
                        dve.tensor_tensor(ccv[:], ccv[:], take(8), ALU.min).then_inc(alu_done, 1)
                        if not is0(i) and f in TAKE:
                            finish(i - 1, TAKE[f])

                def finish(i, q):
                    dve.wait_ge(o_ready, i * OQ + (q + 1))
                    if q == 0:
                        dve.wait_ge(ld_x1, i * 16 + 16)
                    x = x1[:, q * OT:(q + 1) * OT]
                    dve.tensor_tensor(x, ps_o[:, q % 2], x, ALU.add).then_inc(o_done, 1)

                dve.sem_inc(alu_done, ENDS)
                steps(dve, NI, step)
                for k in range(ENDS):
                    end(NI - 1, FT - 1, 1, k, NI * FT * DV + k)
                for q in range(OQ):
                    finish(NI - 1, q)


def build(nc, io):
    with ExitStack() as ctx:
        s = Shared(nc, ctx, io)
        stage_prepare(s)
        stage_gnn(s)
        stage_norm(s)
        stage_tropical(s)
        stage_ffn(s)


def kernel(**inputs):
    import ml_dtypes
    import numpy as np
    import concourse.bacc as bacc
    from concourse.bass_utils import run_bass_kernel_spmd

    arrays = {name: np.ascontiguousarray(a) for name, a in inputs.items()}
    for name, a in arrays.items():
        if a.ndim == 0:
            arrays[name] = a.reshape(1)
    arrays["ident"] = np.eye(P, dtype=np.float32)
    arrays["sel"] = np.ascontiguousarray(np.broadcast_to(
        np.tile(np.eye(UNIT), (PARTS, 1))[:, :, None], (SEL, UNIT, P))).astype(ml_dtypes.bfloat16)
    nc = bacc.Bacc("TRN2", target_bir_lowering=False, num_devices=1)
    io = {name: nc.dram_tensor(f"in_{name}", a.shape, mybir.dt.from_np(a.dtype), kind="ExternalInput").ap()
          for name, a in arrays.items()}
    io["out"] = nc.dram_tensor("out_x", arrays["x"].shape, F32, kind="ExternalOutput").ap()
    build(nc, io)
    r = run_bass_kernel_spmd(nc, [{f"in_{name}": a for name, a in arrays.items()}], core_ids=[0])
    return r.results[0]["out_x"]
```
